# Optimizing a Trainium2 kernel written in Bass

```python
import numpy as np
import jax
import jax.numpy as jnp

def _softmax(x, axis=-1):
    return jax.nn.softmax(x, axis=axis)

def _gelu(x):
    return jax.nn.gelu(x, approximate=True)

def _silu(x):
    return jax.nn.silu(x)

def _sigmoid(x):
    return jax.nn.sigmoid(x)

def _layernorm(x, axis=-1, eps=1e-05):
    m = jnp.mean(x, axis=axis, keepdims=True)
    v = jnp.var(x, axis=axis, keepdims=True)
    return (x - m) / jnp.sqrt(v + eps)

def _scatter_add(tgt, idx, src, axis=0):
    return tgt.at[idx].add(src)

def _segment_sum(src, seg, n):
    return jax.ops.segment_sum(src, seg, n)
kernel_name = 'mk_macaron_d1_jaxref_r4_5a853a'

def setup_inputs(seed: int=0):
    np.random.seed(seed)
    _w = jnp.asarray

    def _L0_attn_setup():
        import jax, jax.numpy as jnp
        import numpy as np
        B, S, D, H = (2, 512, 256, 16)
        HD = D // H
        key = jax.random.key(seed)
        ks = jax.random.split(key, 5)
        return {'x': jax.random.normal(ks[0], (B, S, D), dtype=jnp.float32), 'qkv_w': jax.random.normal(ks[1], (3 * D, D), dtype=jnp.float32) * (1.0 / np.sqrt(D)), 'qkv_b': jax.random.normal(ks[2], (3 * D,), dtype=jnp.float32) * 0.02, 'proj_w': jax.random.normal(ks[3], (D, D), dtype=jnp.float32) * (1.0 / np.sqrt(D)), 'proj_b': jax.random.normal(ks[4], (D,), dtype=jnp.float32) * 0.02}
    _L0_attn_in = _L0_attn_setup()

    def _L0_ffn_setup():
        import jax, jax.numpy as jnp
        import numpy as np
        TOP_K = 4
        CAP_FACTOR = 4

        def swiglu(x, w1, w2, w3):
            return jax.nn.silu(x @ w1) * (x @ w3) @ w2
        key = jax.random.key(seed)
        ks = jax.random.split(key, 8)
        B, S, D, H, E = (2, 512, 256, 128, 32)
        Hs = 2 * H
        sd = lambda *sh: 1.0 / np.sqrt(sh[-2])
        x = jax.random.normal(ks[0], (B, S, D), dtype=jnp.float32)
        Wg = jax.random.normal(ks[1], (D, E), dtype=jnp.float32) * (1.0 / np.sqrt(D))
        W1 = jax.random.normal(ks[2], (E, D, H), dtype=jnp.float32) * (1.0 / np.sqrt(D))
        W3 = jax.random.normal(ks[3], (E, D, H), dtype=jnp.float32) * (1.0 / np.sqrt(D))
        W2 = jax.random.normal(ks[4], (E, H, D), dtype=jnp.float32) * (1.0 / np.sqrt(H))
        Ws1 = jax.random.normal(ks[5], (D, Hs), dtype=jnp.float32) * (1.0 / np.sqrt(D))
        Ws3 = jax.random.normal(ks[6], (D, Hs), dtype=jnp.float32) * (1.0 / np.sqrt(D))
        Ws2 = jax.random.normal(ks[7], (Hs, D), dtype=jnp.float32) * (1.0 / np.sqrt(Hs))
        return {'x': x, 'Wg': Wg, 'W1': W1, 'W2': W2, 'W3': W3, 'Ws1': Ws1, 'Ws2': Ws2, 'Ws3': Ws3}
    _L0_ffn_in = _L0_ffn_setup()
    _d = {'L0_attn_x': _L0_attn_in['x'], 'L0_attn_qkv_w': _L0_attn_in['qkv_w'], 'L0_attn_qkv_b': _L0_attn_in['qkv_b'], 'L0_attn_proj_w': _L0_attn_in['proj_w'], 'L0_attn_proj_b': _L0_attn_in['proj_b'], 'L0_ffn_Wg': _L0_ffn_in['Wg'], 'L0_ffn_W1': _L0_ffn_in['W1'], 'L0_ffn_W2': _L0_ffn_in['W2'], 'L0_ffn_W3': _L0_ffn_in['W3'], 'L0_ffn_Ws1': _L0_ffn_in['Ws1'], 'L0_ffn_Ws2': _L0_ffn_in['Ws2'], 'L0_ffn_Ws3': _L0_ffn_in['Ws3']}
    _x0 = _d['L0_attn_x']
    _d['L0_attn_x'] = jax.random.normal(jax.random.fold_in(jax.random.key(seed), 1), (1, 4096, 256), dtype=_x0.dtype)
    del _x0
    return _d

def reference(L0_attn_x, L0_attn_qkv_w, L0_attn_qkv_b, L0_attn_proj_w, L0_attn_proj_b, L0_ffn_Wg, L0_ffn_W1, L0_ffn_W2, L0_ffn_W3, L0_ffn_Ws1, L0_ffn_Ws2, L0_ffn_Ws3):

    def _L0_attn_ref(x, qkv_w, qkv_b, proj_w, proj_b):
        import jax, jax.numpy as jnp
        import numpy as np
        B, S, D, H = (2, 512, 256, 16)
        HD = D // H
        b, s, d = x.shape
        qkv = jnp.einsum('bsd,ed->bse', x, qkv_w) + qkv_b
        qkv = qkv.reshape(b, s, 3, H, HD)
        q = jnp.transpose(qkv[:, :, 0], (0, 2, 1, 3))
        k = jnp.transpose(qkv[:, :, 1], (0, 2, 1, 3))
        v = jnp.transpose(qkv[:, :, 2], (0, 2, 1, 3))
        scale = 1.0 / jnp.sqrt(jnp.asarray(HD, dtype=x.dtype))
        scores = jnp.einsum('bhqe,bhke->bhqk', q, k) * scale
        attn = jax.nn.softmax(scores, axis=-1)
        out = jnp.einsum('bhqk,bhke->bhqe', attn, v)
        out = jnp.transpose(out, (0, 2, 1, 3)).reshape(b, s, d)
        out = jnp.einsum('bsd,ed->bse', out, proj_w) + proj_b
        return out

    def _L0_ffn_ref(x, Wg, W1, W2, W3, Ws1, Ws2, Ws3):
        import jax, jax.numpy as jnp
        import numpy as np
        TOP_K = 4
        CAP_FACTOR = 4

        def swiglu(x, w1, w2, w3):
            return jax.nn.silu(x @ w1) * (x @ w3) @ w2
        B, S, D = x.shape
        E = Wg.shape[1]
        T = B * S
        xf = x.reshape(T, D)
        scores = jax.nn.softmax(xf @ Wg, axis=-1)
        weights, indices = jax.lax.top_k(scores, TOP_K)
        P = T * TOP_K
        pair_expert = indices.reshape(-1)
        pair_token = jnp.repeat(jnp.arange(T), TOP_K)
        pair_weight = weights.reshape(-1).astype(xf.dtype)
        C = CAP_FACTOR * P // E
        y = jnp.zeros_like(xf)
        for e in range(E):
            pos = jnp.nonzero(pair_expert == e, size=C, fill_value=P)[0]
            valid = pos < P
            safe = jnp.minimum(pos, P - 1)
            tok = jnp.where(valid, pair_token[safe], 0)
            w = jnp.where(valid, pair_weight[safe], 0.0)
            xg = xf[tok]
            out = swiglu(xg, W1[e], W2[e], W3[e]) * w[:, None]
            y = y.at[tok].add(out)
        z = swiglu(xf, Ws1, Ws2, Ws3)
        return (y + z).reshape(B, S, D)
    x = L0_attn_x
    x = x + 0.5 * _L0_ffn_ref(_layernorm(x, axis=-1), L0_ffn_Wg, L0_ffn_W1, L0_ffn_W2, L0_ffn_W3, L0_ffn_Ws1, L0_ffn_Ws2, L0_ffn_Ws3)
    x = x + _L0_attn_ref(_layernorm(x, axis=-1), L0_attn_qkv_w, L0_attn_qkv_b, L0_attn_proj_w, L0_attn_proj_b)
    x = x + 0.5 * _L0_ffn_ref(_layernorm(x, axis=-1), L0_ffn_Wg, L0_ffn_W1, L0_ffn_W2, L0_ffn_W3, L0_ffn_Ws1, L0_ffn_Ws2, L0_ffn_Ws3)
    return x

_drawn_inputs = setup_inputs


def setup_inputs(seed=0):
    import zlib

    import numpy as np

    out = dict(_drawn_inputs(seed))
    spreads = {}
    factors = {'L0_attn_proj_b': 3.162}
    for name, (base, spread) in spreads.items():
        noise = np.random.default_rng([zlib.crc32(name.encode()), seed]).standard_normal(out[name].shape)
        drawn = base * np.exp(spread * noise) if base else spread * noise
        out[name] = jnp.asarray(drawn.astype(out[name].dtype))
    for name, factor in factors.items():
        out[name] = (out[name] * factor).astype(out[name].dtype)
    return out
```

```python
import numpy as np
import concourse.bass as bass
from concourse import mybir
from contextlib import ExitStack

F32 = mybir.dt.float32
BF16 = mybir.dt.bfloat16
I32 = mybir.dt.int32
ACT = mybir.ActivationFunctionType
ALU = mybir.AluOpType
AX = mybir.AxisListType.X

P = 128
T = 4096
D = 256
DC = D // P
NT = T // P
E = 32
H = 128
HS = 256
HSC = HS // P
TOPK = 4
CAP = 4 * T * TOPK // E
NJ = T * TOPK // P + E
BIG = 32768.0
WCOLS = DC * 2 * H + D
EPS = 1e-5
BLK = 512
NB = T // BLK
TPB = BLK // P
NH = 16
HD = D // NH
SCALE = HD ** -0.5
NPART = 3
KROWS = 6 * HD
QROWS = KROWS + NPART
SAFE = 70.0
LIMIT = SAFE / SCALE


def semaphores(nc, stage, ctx):
    made = {}

    def give_back():
        nc.clear_and_free_semaphores(list(made.values()))
        nc.all_engine_barrier()

    if ctx is not None:
        ctx.callback(give_back)

    def sem(name):
        if name not in made:
            made[name] = nc.alloc_semaphore(f"{stage}_{name}")
        return made[name]

    return sem


class Chain:

    def __init__(self, eng, sem):
        self.eng, self.sem, self.n, self.base = eng, sem, 0, 0

    def mark(self, ins):
        self.n += 1
        ins.then_inc(self.sem, 1)

    def join(self):
        self.eng.wait_ge(self.sem, self.base + self.n)

    def link(self, ins):
        self.mark(ins)
        self.join()


class Loop:

    def __init__(self, chain, i, count, each):
        self.chain, self.count, self.each = chain, count, each
        self.start = chain.n
        chain.base = chain.base + i * each

    def close(self):
        c = self.chain
        assert c.n - self.start == self.each, (c.n - self.start)
        c.base = 0
        c.n = self.start + self.each * self.count


def skewed(eng, count, unroll, step):
    first = 2
    def peeled(j):
        step(j, j % unroll, lambda d: (j + d) // unroll)

    def inside(i, u):
        step(i * unroll + (first + u), (first + u) % unroll, lambda d: i + (first + u + d) // unroll)

    for j in range(-2, first):
        peeled(j)
    rounds = (count - 2 - first) // unroll
    with eng.Fori(0, rounds) as i:
        for u in range(unroll):
            inside(i, u)
    for j in range(first + rounds * unroll, count + 1):
        peeled(j)


def carried(eng, seen):
    eng.sem_inc(seen, 1)


def has(j, d, count):
    return 0 <= j + d < count if isinstance(j, int) else True


def build(nc, a, out):
    ctx = ExitStack()
    with ctx:
        sem = semaphores(nc, "k", None)

        def sb(name, shape, dt, c=ctx):
            return c.enter_context(nc.sbuf_tensor(name, shape, dt))

        def pb(name, shape, dt, c):
            return c.enter_context(nc.psum_tensor(name, shape, dt))

        def dram(name, shape, dt):
            return nc.dram_tensor(name, shape, dt, kind="Internal").ap()

        xn_d = dram("xn_d", (T, D), F32)
        pair_d = dram("pair_d", (NJ * P, D), F32)
        x_d = dram("x_d", (T, D), F32)
        part_d = dram("part_d", (NPART, 2 * D, T), BF16)
        shift_d = dram("shift_d", (NPART, NH, T), BF16)
        head_d = dram("head_d", (NB, 2, D, BLK), F32)

        WE = sb("WE", [P, E, WCOLS], F32)
        RA = sb("RA", [P, NT * D], F32)
        RB = sb("RB", [P, NT * D], F32)
        X = RA[:, :].rearrange("p (t d) -> p t d", t=NT)
        XNT = RB[:, :].rearrange("p (c t) -> p c t", c=DC)
        ident = sb("ident", [P, P], F32)

        with nc.Block() as block:
            @block.sync
            def _(sp):
                sp.dma_start(X, a["x"][0].rearrange("(t p) d -> p t d", p=P)).then_inc(sem("x_in"), 16)
                sp.wait_ge(sem("x_in"), 16)

            @block.gpsimd
            def _(pool):
                pool.memset(ident[:, :], 0.0).then_inc(sem("ident0"), 1)
                pool.wait_ge(sem("ident0"), 1)
                pool.affine_select(out=ident[:, :], in_=ident[:, :], compare_op=ALU.not_equal, fill=1.0,
                                   base=0, pattern=[[-1, P]], channel_multiplier=1).then_inc(sem("ident0"), 1)

            @block.scalar
            def _(act):
                for c in range(DC):
                    for n, w in enumerate(("W1", "W3")):
                        act.dma_start(WE[:, :, (2 * c + n) * H:(2 * c + n + 1) * H],
                                      a[w][:, c * P:(c + 1) * P, :].rearrange("e p h -> p e h"))\
                           .then_inc(sem("we_in"), 16)
                act.dma_start(WE[:, :, DC * 2 * H:], a["W2"].rearrange("e h d -> h e d")).then_inc(sem("we_in"), 16)

        ffn(nc, a, 0, locals())
        attention(nc, a, locals())
        ffn(nc, a, 1, locals())
        ffn_out(nc, a, out, locals())


def normalise_stats(v, link, X, stats, mean, rstd, tmp, var, act_sem, sqrt_sem):
    with v.Fori(0, NT // 4) as i:
        for u in range(4):
            last = v.bn_stats(stats[:, i * 4 + u, :], X[:, i * 4 + u, :])
            last.then_inc(act_sem, 1)
    v.wait_ge(act_sem, NT)
    link(v.tensor_tensor(mean[:, :], stats[:, :, 1], stats[:, :, 4], ALU.add))
    link(v.tensor_tensor(tmp[:, :], stats[:, :, 1], stats[:, :, 4], ALU.subtract))
    link(v.tensor_scalar(mean[:, :], mean[:, :], 0.5, None, ALU.mult))
    link(v.tensor_scalar(tmp[:, :], tmp[:, :], 0.5, None, ALU.mult))
    link(v.tensor_tensor(tmp[:, :], tmp[:, :], tmp[:, :], ALU.mult))
    link(v.tensor_tensor(var[:, :], stats[:, :, 2], stats[:, :, 5], ALU.add))
    link(v.tensor_scalar(var[:, :], var[:, :], 1.0 / D, None, ALU.mult))
    link(v.tensor_tensor(var[:, :], var[:, :], tmp[:, :], ALU.add))
    link(v.tensor_scalar(var[:, :], var[:, :], EPS, None, ALU.add))
    v.sem_inc(sqrt_sem, 1)
    v.wait_ge(sqrt_sem, 2)
    link(v.reciprocal(rstd[:, :], tmp[:, :]))


def ffn(nc, a, L, env):
    sb, pb = env["sb"], env["pb"]
    X, XNT, WE, ident = env["X"], env["XNT"], env["WE"], env["ident"]
    xn_d, pair_d = env["xn_d"], env["pair_d"]

    with ExitStack() as keep:
        sem = semaphores(nc, f"f{L}", keep)
        slot_token = sb(f"slot_token{L}", [P, NJ], I32, keep)
        tile_expert = sb(f"tile_expert{L}", [1, NJ], I32, keep)
        pair_slot = sb(f"pair_slot{L}", [P, NT, TOPK], I32, keep)
        pair_weight = sb(f"pair_weight{L}", [P, NT, TOPK], F32, keep)
        route(nc, a, L, sem, sb, pb, X, XNT, ident, xn_d, slot_token, tile_expert, pair_slot, pair_weight)
        experts(nc, L, sem, sb, pb, WE, ident, xn_d, pair_d, slot_token, tile_expert, env)
        combine(nc, a, L, sem, sb, pb, X, XNT, pair_d, pair_slot, pair_weight, env)


def route(nc, a, L, sem, sb, pb, X, XNT, ident, xn_d, slot_token, tile_expert, pair_slot, pair_weight):
    U = 4
    with ExitStack() as c:
        stats = sb(f"stats{L}", [P, NT, 6], F32, c)
        mean = sb(f"mean{L}", [P, NT], F32, c)
        rstd = sb(f"rstd{L}", [P, NT], F32, c)
        var = sb(f"var{L}", [P, NT], F32, c)
        tmp = sb(f"tmp{L}", [P, NT], F32, c)
        wg = sb(f"wg{L}", [P, DC, E], F32, c)
        xn = sb(f"xn{L}", [P, U, D], F32, c)
        xnt = sb(f"xnt{L}", [P, 2, DC, P], F32, c)
        SC = sb(f"SC{L}", [P, NT, E], F32, c)
        A1 = sb(f"A1{L}", [P, NT, E], F32, c)
        A2 = sb(f"A2{L}", [P, NT, E], F32, c)
        TW = sb(f"TW{L}", [P, NT, E], F32, c)
        M = sb(f"M{L}", [P, NT, E], BF16, c)
        R = sb(f"R{L}", [P, NT + 1, E], BF16, c)
        top8 = sb(f"top8{L}", [P, NT, 8], F32, c)
        slot8 = sb(f"slot8{L}", [P, NT, 8], F32, c)
        row1 = sb(f"row1{L}", [P, NT], F32, c)
        row2 = sb(f"row2{L}", [P, NT], F32, c)
        base = sb(f"base{L}", [P, E], F32, c)
        earlier = sb(f"earlier{L}", [P, P], BF16, c)
        upto = sb(f"upto{L}", [E, 2 * E], BF16, c)
        ones = sb(f"ones{L}", [P, P], BF16, c)
        zeros = sb(f"zeros{L}", [P, P], BF16, c)
        zrow = sb(f"zrow{L}", [P, 2 * NJ], BF16, c)
        cnt_f = sb(f"cnt_f{L}", [E, 1], F32, c)
        cnt_i = sb(f"cnt_i{L}", [E, 1], I32, c)
        tiles_bf = sb(f"tiles_bf{L}", [E, 1], BF16, c)
        tiles_f = sb(f"tiles_f{L}", [E, 1], F32, c)
        spread = sb(f"spread{L}", [E, 2 * E], BF16, c)
        end_col = sb(f"end_col{L}", [E, 1], F32, c)
        past = sb(f"past{L}", [E, NJ], BF16, c)
        iota_i = sb(f"iota_i{L}", [P, NJ], I32, c)
        iota_b = sb(f"iota_b{L}", [P, NJ], BF16, c)
        iota_f = sb(f"iota_f{L}", [P, NJ], F32, c)
        part_i = sb(f"part_i{L}", [P, 1], I32, c)
        part_f = sb(f"part_f{L}", [P, 1], F32, c)
        pf = sb(f"pf{L}", [P, NT, TOPK], F32, c)
        pv = sb(f"pv{L}", [P, NT, TOPK], F32, c)
        pi = sb(f"pi{L}", [P, NT, TOPK], I32, c)
        lo_f = sb(f"lo_f{L}", [P, NT, TOPK], F32, c)
        hi_f = sb(f"hi_f{L}", [P, NT, TOPK], F32, c)
        at_row = sb(f"at_row{L}", [P, TOPK, P], BF16, c)
        at_tile = sb(f"at_tile{L}", [P, TOPK, 2, NJ], BF16, c)
        tok_f = sb(f"tok_f{L}", [P, NJ], F32, c)
        psT = [pb(f"psT{i}_{L}", [P, DC * P], F32, c) for i in range(2)]
        psL = pb(f"psL{L}", [P, NT * E], F32, c)
        psR = pb(f"psR{L}", [P, NT * E], F32, c)
        psI = pb(f"psI{L}", [P, 512], F32, c)
        psM = pb(f"psM{L}", [P, 512], F32, c)

        def by_tile(ap):
            return ap.rearrange("p (t e) -> p t e", e=E)

        def over_experts(ap):
            return ap.unsqueeze(2).to_broadcast([P, NT, E])

        with nc.Block() as block:
            @block.sync
            def _(sp):
                sp.dma_start(wg[:, :, :], a["Wg"].rearrange("(c p) e -> p c e", p=P)).then_inc(sem("wg"), 16)
                for u in range(U):
                    sp.sem_inc(sem(f"xn_stored{u}"), 16)
                with sp.Fori(0, NT // U) as i:
                    for u in range(U):
                        t = i * U + u
                        sp.wait_ge(sem("xn_ready"), t + 1)
                        sp.dma_start(xn_d[bass.ds(t * P, P), :], xn[:, u, :]).then_inc(sem(f"xn_stored{u}"), 16)
                for u in range(U):
                    sp.wait_ge(sem(f"xn_stored{u}"), 16 * (1 + NT // U))

            @block.gpsimd
            def _(pool):
                own = Chain(pool, sem("pool"))
                pool.memset(ones[:, :], 1.0)
                pool.memset(zeros[:, :], 0.0)
                pool.memset(zrow[:, :], 0.0)
                pool.memset(earlier[:, :], 1.0).then_inc(sem("consts"), 1)
                pool.memset(upto[:, :], 1.0).then_inc(sem("consts"), 1)
                pool.memset(R[:, 0, :], 0.0).then_inc(sem("consts"), 1)
                pool.wait_ge(sem("consts"), 3)
                pool.affine_select(out=earlier[:, :], in_=earlier[:, :], compare_op=ALU.is_gt, fill=0.0,
                                   base=0, pattern=[[1, P]], channel_multiplier=-1).then_inc(sem("consts"), 1)
                pool.affine_select(out=upto[:, 0:E], in_=upto[:, 0:E], compare_op=ALU.is_ge, fill=0.0,
                                   base=0, pattern=[[1, E]], channel_multiplier=-1).then_inc(sem("consts"), 1)
                pool.affine_select(out=upto[:, E:2 * E], in_=upto[:, E:2 * E], compare_op=ALU.is_gt, fill=0.0,
                                   base=0, pattern=[[1, E]], channel_multiplier=-1).then_inc(sem("consts"), 1)
                pool.iota(iota_i[:, :], pattern=[[1, NJ]], base=0, channel_multiplier=0).then_inc(sem("consts"), 1)
                pool.iota(part_i[:, :], pattern=[[0, 1]], base=0, channel_multiplier=1).then_inc(sem("consts"), 1)
                with pool.Fori(0, NT // U) as i:
                    for u in range(U):
                        t = i * U + u
                        pool.wait_ge(sem("xnt_ready"), t + 1)
                        pool.tensor_copy(XNT[:, :, bass.ds(t * P, P)], xnt[:, u % 2, :, :]).then_inc(sem("xnt_kept"), 1)

            @block.scalar
            def _(act):
                act.wait_ge(sem("sqrt"), 1)
                act.activation(tmp[:, :], var[:, :], ACT.Sqrt).then_inc(sem("sqrt"), 1)
                act.sem_inc(sem("xnt_kept"), 2)
                with act.Fori(0, NT // U) as i:
                    for u in range(U):
                        t = i * U + u
                        act.wait_ge(sem("turned"), t + 1 + U)
                        act.wait_ge(sem("xnt_kept"), t + 1)
                        act.wait_ge(sem("routed"), t + 1)
                        act.activation(xnt[:, u % 2, :, :].rearrange("p c t -> p (c t)"), psT[u % 2][:, :], ACT.Copy)\
                           .then_inc(sem("xnt_ready"), 1)
                act.wait_ge(sem("shifted"), 1)
                act.activation(SC[:, :, :], SC[:, :, :], ACT.Exp).then_inc(sem("exped"), 1)

            @block.tensor
            def _(pe):
                pe.wait_ge(sem("wg"), 16)
                pe.sem_inc(sem("turned"), U)
                pe.sem_inc(sem("routed"), 2)

                def turn(t, u):
                    pe.wait_ge(sem("xn_ready"), t + 1)
                    if not isinstance(t, int) or t >= 2:
                        pe.wait_ge(sem("xnt_ready"), t - 1)
                    for c in range(DC):
                        last = pe.transpose(psT[u % 2][:, c * P:(c + 1) * P], xn[:, u, c * P:(c + 1) * P], ident[:, :])
                    last.then_inc(sem("turned"), 1)

                def logits(t, u):
                    pe.wait_ge(sem("xnt_ready"), t + 1)
                    for c in range(DC):
                        last = pe.matmul(psL[:, bass.ds(t * E, E)], xnt[:, u % 2, c, :], wg[:, c, :],
                                         start=(c == 0), stop=(c == DC - 1))
                    last.then_inc(sem("routed"), 1)

                for t in range(U):
                    turn(t, t)
                    if t:
                        logits(t - 1, t - 1)
                with pe.Fori(1, NT // U) as i:
                    for u in range(U):
                        turn(i * U + u, u)
                        logits(i * U + (u - 1), (u - 1) % U)
                logits(NT - 1, U - 1)

                pe.wait_ge(sem("masked"), 1)
                Mf, Rf = M[:, :, :].rearrange("p t e -> p (t e)"), R[:, 0:NT, :].rearrange("p t e -> p (t e)")
                for b in range(NT * E // 512):
                    w = slice(b * 512, (b + 1) * 512)
                    pe.matmul(psR[:, w], earlier[:, :], Mf[:, w], start=True, stop=False)
                    pe.matmul(psR[:, w], ones[:, :], Rf[:, w], start=False, stop=True)
                pe.matmul(psM[0:E, 0:1], R[:, NT, :], ones[:, 0:1], start=True, stop=True).then_inc(sem("ranked"), 1)
                pe.wait_ge(sem("sized"), 1)
                pe.matmul(psM[:, 64:128], ones[0:E, :], spread[:, :], start=True, stop=True)
                pe.matmul(psM[0:E, 1:2], upto[:, 0:E], tiles_bf[:, :], start=True, stop=True).then_inc(sem("ends"), 1)
                pe.wait_ge(sem("past"), 1)
                pe.matmul(psM[0:1, 128:128 + NJ], ones[0:E, 0:1], past[:, :], start=True, stop=True).then_inc(sem("owners"), 1)
                pe.matmul(psI[:, 0:2 * NJ], zeros[:, :], zrow[:, :], start=True, stop=False)
                pe.sem_inc(sem("placed"), TOPK)
                with pe.Fori(0, NT) as i:
                    for k in range(TOPK):
                        n = i * TOPK + k
                        pe.wait_ge(sem("onehot"), n + 1)
                        pe.matmul(psI[:, 0:2 * NJ], at_row[:, k, :], at_tile[:, k, :, :].rearrange("p a j -> p (a j)"),
                                  start=False, stop=False, skip_group_check=True).then_inc(sem("placed"), 1)
                pe.matmul(psI[:, 0:2 * NJ], zeros[:, :], zrow[:, :], start=False, stop=True).then_inc(sem("all_placed"), 1)

            @block.vector
            def _(v):
                own = Chain(v, sem("dve"))
                link, mark, join = own.link, own.mark, own.join
                normalise_stats(v, link, X, stats, mean, rstd, tmp, var, sem("stats"), sem("sqrt"))
                with v.Fori(0, NT // U) as i:
                    for u in range(U):
                        t = i * U + u
                        v.wait_ge(sem("turned"), t + 1)
                        v.wait_ge(sem(f"xn_stored{u}"), i * 16 + 16)
                        v.tensor_scalar(xn[:, u, :], X[:, t, :], mean[:, bass.ds(t, 1)], rstd[:, bass.ds(t, 1)],
                                        ALU.subtract, ALU.mult).then_inc(sem("xn_ready"), 1)
                v.wait_ge(sem("consts"), 8)
                mark(v.tensor_copy(iota_f[:, :], iota_i[:, :]))
                mark(v.tensor_copy(iota_b[:, :], iota_i[:, :]))
                mark(v.tensor_copy(part_f[:, :], part_i[:, :]))

                v.wait_ge(sem("routed"), 2 + NT)
                link(v.tensor_reduce(row1[:, :], by_tile(psL[:, :]), AX, ALU.max))
                v.tensor_tensor(SC[:, :, :], by_tile(psL[:, :]), over_experts(row1[:, :]), ALU.subtract)\
                 .then_inc(sem("shifted"), 1)
                v.wait_ge(sem("exped"), 1)
                link(v.tensor_reduce(row2[:, :], SC[:, :, :], AX, ALU.add))
                link(v.reciprocal(row2[:, :], row2[:, :]))
                link(v.tensor_tensor(SC[:, :, :], SC[:, :, :], over_experts(row2[:, :]), ALU.mult))

                for t in range(NT):
                    mark(v.max(top8[:, t, :], SC[:, t, :]))
                join()
                link(v.memset(top8[:, :, TOPK:], -1.0))
                for t in range(NT):
                    mark(v.match_replace(A1[:, t, :], top8[:, t, :], SC[:, t, :], -2.0))
                join()
                link(v.tensor_scalar(M[:, :, :], A1[:, :, :], -1.5, None, ALU.is_lt))
                for t in range(NT):
                    last = v.tensor_tensor(R[:, t + 1, :], R[:, t, :], M[:, t, :], ALU.add)
                    if t < NT - 1:
                        link(last)
                last.then_inc(sem("masked"), 1)

                v.wait_ge(sem("ranked"), 1)
                link(v.tensor_scalar(cnt_f[:, :], psM[0:E, 0:1], float(CAP), float(P - 1), ALU.min, ALU.add))
                link(v.tensor_copy(cnt_i[:, :], cnt_f[:, :]))
                link(v.tensor_scalar(cnt_i[:, :], cnt_i[:, :], 7, None, ALU.arith_shift_right))
                link(v.tensor_copy(tiles_f[:, :], cnt_i[:, :]))
                mark(v.tensor_copy(tiles_bf[:, :], tiles_f[:, :]))
                join()
                v.tensor_scalar(spread[:, :], upto[:, :], tiles_f[:, :], None, ALU.mult).then_inc(sem("sized"), 1)
                v.wait_ge(sem("ends"), 1)
                link(v.tensor_copy(end_col[:, :], psM[0:E, 1:2]))
                link(v.tensor_scalar(base[:, :], psM[:, 64 + E:64 + 2 * E], float(P), None, ALU.mult))
                v.tensor_scalar(past[:, :], iota_f[0:E, :], end_col[:, :], None, ALU.is_ge).then_inc(sem("past"), 1)

                link(v.tensor_scalar(A1[:, :, :], by_tile(psR[:, :]), float(CAP), None, ALU.is_lt))
                link(v.tensor_tensor(A1[:, :, :], A1[:, :, :], M[:, :, :], ALU.mult))
                mark(v.tensor_tensor(TW[:, :, :], SC[:, :, :], A1[:, :, :], ALU.mult))
                link(v.tensor_tensor(A2[:, :, :], by_tile(psR[:, :]), base[:, :].unsqueeze(1).to_broadcast([P, NT, E]), ALU.add))
                link(v.tensor_scalar(A2[:, :, :], A2[:, :, :], -1.0, BIG, ALU.mult, ALU.add))
                link(v.tensor_tensor(A2[:, :, :], A2[:, :, :], A1[:, :, :], ALU.mult))
                for t in range(NT):
                    mark(v.max(slot8[:, t, :], A2[:, t, :]))
                join()
                link(v.tensor_scalar(pv[:, :, :], slot8[:, :, 0:TOPK], 0.0, None, ALU.is_gt))
                link(v.tensor_scalar(pf[:, :, :], slot8[:, :, 0:TOPK], -1.0, BIG, ALU.mult, ALU.add))
                link(v.tensor_tensor(pf[:, :, :], pf[:, :, :], pv[:, :, :], ALU.mult))
                link(v.tensor_copy(pair_slot[:, :, :], pf[:, :, :]))
                link(v.tensor_scalar(pi[:, :, :], pair_slot[:, :, :], P - 1, None, ALU.bitwise_and))
                link(v.tensor_copy(lo_f[:, :, :], pi[:, :, :]))
                link(v.tensor_scalar(pi[:, :, :], pair_slot[:, :, :], 7, None, ALU.arith_shift_right))
                link(v.tensor_copy(hi_f[:, :, :], pi[:, :, :]))
                link(v.tensor_scalar(pv[:, :, :], pv[:, :, :], -1000.0, 1000.0, ALU.mult, ALU.add))
                link(v.tensor_tensor(hi_f[:, :, :], hi_f[:, :, :], pv[:, :, :], ALU.add))

                with v.Fori(0, NT) as i:
                    for k in range(TOPK):
                        n = i * TOPK + k
                        v.wait_ge(sem("placed"), n + 1)
                        lo, hi = lo_f[:, bass.ds(i, 1), k], hi_f[:, bass.ds(i, 1), k]
                        v.tensor_scalar(at_row[:, k, :], iota_b[:, 0:P], lo, None, ALU.is_equal)
                        v.tensor_scalar(at_tile[:, k, 0, :], iota_b[:, :], hi, iota_f[:, bass.ds(i, 1)], ALU.is_equal, ALU.mult)
                        v.tensor_scalar(at_tile[:, k, 1, :], iota_b[:, :], hi, part_f[:, :], ALU.is_equal, ALU.mult)\
                         .then_inc(sem("onehot"), 1)

                for k in range(TOPK):
                    link(v.tensor_tensor(A1[:, :, :], A2[:, :, :], over_experts(slot8[:, :, k]), ALU.is_equal))
                    link(v.tensor_tensor(A1[:, :, :], A1[:, :, :], TW[:, :, :], ALU.mult))
                    link(v.tensor_reduce(pair_weight[:, :, k], A1[:, :, :], AX, ALU.add))
                link(v.tensor_scalar(pair_weight[:, :, :], pair_weight[:, :, :], 0.5, None, ALU.mult))
                v.wait_ge(sem("owners"), 1)
                link(v.tensor_scalar(tile_expert[:, :], psM[0:1, 128:128 + NJ], float(E - 1), None, ALU.min))
                v.wait_ge(sem("all_placed"), 1)
                link(v.tensor_scalar(tok_f[:, :], psI[:, 0:NJ], float(P), None, ALU.mult))
                link(v.tensor_tensor(tok_f[:, :], tok_f[:, :], psI[:, NJ:2 * NJ], ALU.add))
                link(v.tensor_copy(slot_token[:, :], tok_f[:, :]))


def experts(nc, L, sem, sb, pb, WE, ident, xn_d, pair_d, slot_token, tile_expert, env):
    U = 4
    gathered = [env["sem"](f"gathered{u}") for u in range(U)]
    with ExitStack() as c:
        index = sb(f"index{L}", [P, U], I32, c)
        xg = sb(f"xg{L}", [P, U, D], F32, c)
        xgt = sb(f"xgt{L}", [P, 2, D], F32, c)
        gate = sb(f"gate{L}", [P, 2, H], F32, c)
        hid = sb(f"hid{L}", [P, 2, H], F32, c)
        hidt = sb(f"hidt{L}", [P, 2, H], F32, c)
        ob = sb(f"ob{L}", [P, U, D], F32, c)
        psX = [pb(f"psX{i}_{L}", [P, D], F32, c) for i in range(2)]
        psH = [pb(f"psH{i}_{L}", [P, 2 * H], F32, c) for i in range(2)]
        psG = [pb(f"psG{i}_{L}", [P, H], F32, c) for i in range(2)]
        psO = [pb(f"psO{i}_{L}", [P, D], F32, c) for i in range(2)]

        with nc.Block() as block:
            @block.gpsimd
            def _(pool):
                with pool.Fori(0, NJ // U) as i:
                    for u in range(U):
                        j = i * U + u
                        pool.wait_ge(sem("x_turned"), j + 1)
                        pool.tensor_copy(index[:, u:u + 1], slot_token[:, bass.ds(j, 1)]).then_inc(sem("indexed"), 1)
                        pool.wait_ge(sem("indexed"), j + 1)
                        pool.sem_inc(sem("index_seen"), 1)
                        pool.indirect_dma_start(xg[:, u, :], None, xn_d, bass.IndirectOffsetOnAxis(ap=index[:, u:u + 1], axis=0))\
                            .then_inc(gathered[u], 16)

            @block.tensor
            def _(pe):
                if L == 0:
                    pe.wait_ge(env["sem"]("we_in"), 16 * 5)
                pe.sem_inc(sem("x_turned"), U)

                def step(j, s, lap):
                    if has(j, 2, NJ):
                        pe.wait_ge(gathered[(s + 2) % U], lap(2) * 16 + (16 + L * 16 * NJ // U))
                        if has(j, 0, NJ):
                            pe.wait_ge(sem("xgt_ready"), j + 1)
                        for c in range(DC):
                            last = pe.transpose(psX[s % 2][:, c * P:(c + 1) * P], xg[:, (s + 2) % U, c * P:(c + 1) * P], ident[:, :])
                        last.then_inc(sem("x_turned"), 1)
                    if has(j, 1, NJ):
                        e = pe.value_load(tile_expert[0:1, bass.ds(j + 1, 1)], min_val=0, max_val=E - 1)
                        pe.wait_ge(sem("xgt_ready"), j + 2)
                        if has(j, -1, NJ):
                            pe.wait_ge(sem("hid_ready"), j)
                        for c in range(DC):
                            last = pe.matmul(psH[(s + 1) % 2][:, :], xgt[:, (s + 1) % 2, c * P:(c + 1) * P],
                                             WE[:, e, c * 2 * H:(c + 1) * 2 * H], start=(c == 0), stop=(c == DC - 1))
                        last.then_inc(sem("up"), 1)
                    if has(j, 0, NJ):
                        pe.wait_ge(sem("hid_ready"), j + 1)
                        if has(j, -2, NJ):
                            pe.wait_ge(sem("hidt_ready"), j - 1)
                        pe.transpose(psG[s % 2][:, :], hid[:, s % 2, :], ident[:, :]).then_inc(sem("h_turned"), 1)
                    if has(j, -1, NJ):
                        e = pe.value_load(tile_expert[0:1, bass.ds(j - 1, 1)], min_val=0, max_val=E - 1)
                        pe.wait_ge(sem("hidt_ready"), j)
                        if has(j, -3, NJ):
                            pe.wait_ge(sem("ob_ready"), j - 2)
                        pe.matmul(psO[(s - 1) % 2][:, :], hidt[:, (s - 1) % 2, :], WE[:, e, DC * 2 * H:],
                                  start=True, stop=True).then_inc(sem("down"), 1)

                skewed(pe, NJ, U, step)

            @block.vector
            def _(v):
                def step(j, s, lap):
                    if has(j, 2, NJ):
                        v.wait_ge(sem("x_turned"), j + 3 + U)
                        if has(j, 0, NJ):
                            v.wait_ge(sem("up"), j + 1)
                        v.tensor_copy(xgt[:, s % 2, :], psX[s % 2][:, :]).then_inc(sem("xgt_ready"), 1)
                    if has(j, 1, NJ):
                        v.wait_ge(sem("gated"), j + 2)
                        if has(j, -1, NJ):
                            v.wait_ge(sem("h_turned"), j)
                        v.tensor_tensor(hid[:, (s + 1) % 2, :], gate[:, (s + 1) % 2, :], psH[(s + 1) % 2][:, H:], ALU.mult)\
                         .then_inc(sem("hid_ready"), 1)

                skewed(v, NJ, U, step)

            @block.scalar
            def _(act):
                for u in range(U):
                    act.sem_inc(sem(f"stored{u}"), 16)

                def step(j, s, lap):
                    if has(j, 1, NJ):
                        act.wait_ge(sem("up"), j + 2)
                        if has(j, -1, NJ):
                            act.wait_ge(sem("hid_ready"), j)
                        act.activation(gate[:, (s + 1) % 2, :], psH[(s + 1) % 2][:, 0:H], ACT.Silu).then_inc(sem("gated"), 1)
                    if has(j, 0, NJ):
                        act.wait_ge(sem("h_turned"), j + 1)
                        if has(j, -2, NJ):
                            act.wait_ge(sem("down"), j - 1)
                        act.activation(hidt[:, s % 2, :], psG[s % 2][:, :], ACT.Copy).then_inc(sem("hidt_ready"), 1)
                    if has(j, -1, NJ):
                        act.wait_ge(sem("down"), j)
                        act.wait_ge(sem(f"stored{(s - 1) % U}"), lap(-1) * 16 + 16)
                        act.activation(ob[:, (s - 1) % U, :], psO[(s - 1) % 2][:, :], ACT.Copy).then_inc(sem("ob_ready"), 1)

                skewed(act, NJ, U, step)

            @block.sync
            def _(sp):
                with sp.Fori(0, NJ // U) as i:
                    for u in range(U):
                        j = i * U + u
                        sp.wait_ge(sem("ob_ready"), j + 1)
                        sp.dma_start(pair_d[bass.ds(j * P, P), :], ob[:, u, :]).then_inc(sem(f"stored{u}"), 16)
                for u in range(U):
                    sp.wait_ge(sem(f"stored{u}"), 16 * (1 + NJ // U))


def combine(nc, a, L, sem, sb, pb, X, XNT, pair_d, pair_slot, pair_weight, env):
    YS = 2 * TOPK
    y_in = [env["sem"](f"y_in{s}") for s in range(YS)]
    with ExitStack() as c:
        ws1 = sb(f"ws1{L}", [P, DC, HS], F32, c)
        ws3 = sb(f"ws3{L}", [P, DC, HS], F32, c)
        ws2 = sb(f"ws2{L}", [P, HSC, D], F32, c)
        index = sb(f"cindex{L}", [P, YS], I32, c)
        Y = sb(f"Y{L}", [P, YS, D], F32, c)
        gate = sb(f"sgate{L}", [P, HSC, BLK], F32, c)
        hid = sb(f"shid{L}", [P, HSC, BLK], F32, c)
        psA = [pb(f"psA{i}_{L}", [P, BLK], F32, c) for i in range(HSC)]
        psB = [pb(f"psB{i}_{L}", [P, BLK], F32, c) for i in range(HSC)]
        psZ = [pb(f"psZ{i}_{L}", [P, D], F32, c) for i in range(2)]

        with nc.Block() as block:
            @block.sync
            def _(sp):
                sp.dma_start(ws1[:, :, :], a["Ws1"].rearrange("(c p) h -> p c h", p=P)).then_inc(sem("ws"), 16)
                sp.dma_start(ws3[:, :, :], a["Ws3"].rearrange("(c p) h -> p c h", p=P)).then_inc(sem("ws"), 16)
                sp.dma_start(ws2[:, :, :], a["Ws2"].rearrange("(c p) d -> p c d", p=P)).then_inc(sem("ws"), 16)

            @block.gpsimd
            def _(pool):
                pool.sem_inc(sem("y_used"), YS)
                with pool.Fori(0, NT // 2) as i:
                    for u in range(2):
                        for k in range(TOPK):
                            s = u * TOPK + k
                            n = i * YS + s
                            pool.wait_ge(sem("y_used"), n + 1)
                            pool.tensor_copy(index[:, s:s + 1], pair_slot[:, bass.ds(i * 2 + u, 1), k]).then_inc(sem("y_indexed"), 1)
                            pool.wait_ge(sem("y_indexed"), n + 1)
                            pool.sem_inc(sem("y_index_seen"), 1)
                            pool.indirect_dma_start(Y[:, s, :], None, pair_d, bass.IndirectOffsetOnAxis(ap=index[:, s:s + 1], axis=0))\
                                .then_inc(y_in[s], 16)

            @block.tensor
            def _(pe):
                pe.wait_ge(sem("ws"), 48)
                pe.sem_inc(sem("z_added"), 2)
                pe.sem_inc(sem("s_hid"), HSC)
                with pe.Fori(0, NB) as b:
                    for m in range(HSC):
                        pe.wait_ge(sem("s_hid"), b * HSC + (m + 1))
                        for ps, w in ((psA, ws1), (psB, ws3)):
                            for c in range(DC):
                                last = pe.matmul(ps[m][:, :], w[:, c, m * P:(m + 1) * P], XNT[:, c, bass.ds(b * BLK, BLK)],
                                                 start=(c == 0), stop=(c == DC - 1))
                        last.then_inc(sem("s_up"), 1)
                    for u in range(TPB):
                        t = b * TPB + u
                        if u == 0:
                            pe.wait_ge(sem("s_hid"), b * HSC + 2 * HSC)
                        pe.wait_ge(sem("z_added"), t + 1)
                        for m in range(HSC):
                            last = pe.matmul(psZ[u % 2][:, :], hid[:, m, u * P:(u + 1) * P], ws2[:, m, :],
                                             start=(m == 0), stop=(m == HSC - 1))
                        last.then_inc(sem("z_ready"), 1)

            @block.scalar
            def _(act):
                with act.Fori(0, NB) as b:
                    for m in range(HSC):
                        act.wait_ge(sem("s_up"), b * HSC + (m + 1))
                        act.wait_ge(sem("s_hid"), b * HSC + (m + 1))
                        act.activation(gate[:, m, :], psA[m][:, :], ACT.Silu).then_inc(sem("s_gate"), 1)

            @block.vector
            def _(v):
                with v.Fori(0, NB) as b:
                    for m in range(HSC):
                        v.wait_ge(sem("s_gate"), b * HSC + (m + 1))
                        v.tensor_tensor(hid[:, m, :], gate[:, m, :], psB[m][:, :], ALU.mult).then_inc(sem("s_hid"), 1)
                    for u in range(TPB):
                        t = b * TPB + u
                        v.wait_ge(sem("z_ready"), t + 1)
                        v.scalar_tensor_tensor(X[:, t, :], psZ[u % 2][:, :], 0.5, X[:, t, :], ALU.mult, ALU.add)\
                         .then_inc(sem("z_added"), 1)
                        v.wait_ge(sem("z_added"), t + 3)
                        for k in range(TOPK):
                            n = t * TOPK + k
                            v.wait_ge(y_in[(u % 2) * TOPK + k], (b * (TPB // 2) + u // 2) * 16 + (16 + L * 16 * NT // 2))
                            v.scalar_tensor_tensor(X[:, t, :], Y[:, (u % 2) * TOPK + k, :], pair_weight[:, bass.ds(t, 1), k],
                                                   X[:, t, :], ALU.mult, ALU.add).then_inc(sem("y_used"), 1)
                            v.wait_ge(sem("y_used"), n + (YS + 1))


def attention(nc, a, env):
    sb, pb = env["sb"], env["pb"]
    X, RA, RB, ident = env["X"], env["RA"], env["RB"], env["ident"]
    x_d, part_d, shift_d, head_d = env["x_d"], env["part_d"], env["shift_d"], env["head_d"]
    V = RB[:, :].rearrange("p (t d) -> p t d", t=NT)

    with ExitStack() as c:
        sem = semaphores(nc, "a", c)
        pwt = sb("pwt", [P, DC, D], F32, c)
        norms = sb("norms", [NH, T], BF16, c)
        key_norm = sb("key_norm", [NH, NB], F32, c)
        key_mean = sb("key_mean", [NH, 1], F32, c)
        safe = sb("safe", [1, 1], I32, c)
        with ExitStack() as c2:
            wt = sb("wt", [P, DC, 3 * D], F32, c2)
            turn_weights(nc, a, sem, sb, pb, ident, wt, pwt)
            project_heads(nc, a, sem, sb, pb, X, V, ident, wt, norms, key_norm, key_mean, x_d, part_d)
        bound_shift(nc, sem, sb, pb, ident, norms, key_norm, key_mean, safe, shift_d)
        exact_shift(nc, sem, sb, pb, RA, ident, safe, part_d, shift_d)
        attend(nc, sem, sb, pb, RA, V, part_d, shift_d, head_d)
        project_out(nc, a, sem, sb, pb, X, pwt, x_d, head_d)


def turn_weights(nc, a, sem, sb, pb, ident, wt, pwt):
    NQ, NP = 3 * D // P, D // P
    with ExitStack() as c:
        raw = sb("raw", [P, NQ + NP, D], F32, c)
        psW = [pb(f"psW{i}", [P, DC, P], F32, c) for i in range(2)]
        with nc.Block() as block:
            @block.sync
            def _(sp):
                sp.dma_start(raw[:, 0:NQ, :], a["qkv_w"].rearrange("(b p) d -> p b d", p=P)).then_inc(sem("raw"), 16)
                sp.dma_start(raw[:, NQ:, :], a["proj_w"].rearrange("(b p) d -> p b d", p=P)).then_inc(sem("raw"), 16)

            @block.tensor
            def _(pe):
                pe.wait_ge(sem("raw"), 32)
                for b in range(NQ + NP):
                    if b >= 2:
                        pe.wait_ge(sem("w_out"), b - 1)
                    for c in range(DC):
                        last = pe.transpose(psW[b % 2][:, c, :], raw[:, b, c * P:(c + 1) * P], ident[:, :])
                    last.then_inc(sem("w_turned"), 1)

            @block.vector
            def _(v):
                for b in range(NQ + NP):
                    v.wait_ge(sem("w_turned"), b + 1)
                    dst = wt[:, :, b * P:(b + 1) * P] if b < NQ else pwt[:, :, (b - NQ) * P:(b - NQ + 1) * P]
                    v.tensor_copy(dst, psW[b % 2][:, :, :]).then_inc(sem("w_out"), 1)


def project_heads(nc, a, sem, sb, pb, X, V, ident, wt, norms, key_norm, key_mean, x_d, part_d):
    NE = 2 * D // P
    with ExitStack() as c:
        stats = sb("astats", [P, NT, 6], F32, c)
        mean = sb("amean", [P, NT], F32, c)
        rstd = sb("arstd", [P, NT], F32, c)
        var = sb("avar", [P, NT], F32, c)
        tmp = sb("atmp", [P, NT], F32, c)
        xn = sb("axn", [P, TPB, D], F32, c)
        xnt = sb("axnt", [P, 2, DC, BLK], F32, c)
        full = sb("full", [P, 2, BLK], F32, c)
        rest = sb("rest", [P, BLK], F32, c)
        parts = sb("parts", [P, 2, NPART, BLK], BF16, c)
        square = sb("square", [P, NE, BLK], BF16, c)
        bias = sb("bias", [P, NE], F32, c)
        vbias = sb("vbias", [P, D], F32, c)
        heads = sb("heads", [P, 2, NH], BF16, c)
        key_sum = sb("key_sum", [P, 2, NB], F32, c)
        mean_f = sb("mean_f", [P, 2], F32, c)
        mean_sq = sb("mean_sq", [P, 2], BF16, c)
        psT = pb("psTa", [P, DC, BLK], F32, c)
        psQ = [pb(f"psQ{i}", [P, BLK], F32, c) for i in range(2)]
        psV = [pb(f"psV{i}", [P, D], F32, c) for i in range(2)]
        psN = [pb(f"psN{i}", [NH, BLK], F32, c) for i in range(2)]

        with nc.Block() as block:
            @block.sync
            def _(sp):
                sp.dma_start(x_d.rearrange("(t p) d -> p t d", p=P), X).then_inc(sem("x_kept"), 16)
                sp.dma_start(bias[:, :], a["qkv_b"][0:2 * D].rearrange("(b p) -> p b", p=P),
                             allow_slow_non_contiguous=True).then_inc(sem("bias"), 16)
                sp.dma_start(vbias[:, :], a["qkv_b"][2 * D:3 * D].partition_broadcast(P)).then_inc(sem("bias"), 16)
                for r in range(2):
                    sp.sem_inc(sem(f"part_stored{r}"), 16)
                with sp.Fori(0, NB) as b:
                    for e in range(NE):
                        sp.wait_ge(sem("split"), b * NE + (e + 1))
                        sp.dma_start(part_d[:, e * P:(e + 1) * P, bass.ds(b * BLK, BLK)].rearrange("a p t -> p a t"),
                                     parts[:, e % 2, :, :]).then_inc(sem(f"part_stored{e % 2}"), 16)
                for r in range(2):
                    sp.wait_ge(sem(f"part_stored{r}"), 16 * (1 + NB * NE // 2))
                sp.wait_ge(sem("x_kept"), 16)

            @block.gpsimd
            def _(pool):
                pool.memset(heads[:, :, :], 1.0).then_inc(sem("heads"), 1)
                pool.wait_ge(sem("heads"), 1)
                pool.affine_select(out=heads[:, :, :], in_=heads[:, :, :], compare_op=ALU.is_ge, fill=0.0,
                                   base=0, pattern=[[P, 2], [-HD, NH]], channel_multiplier=1).then_inc(sem("heads"), 1)
                pool.wait_ge(sem("heads"), 2)
                pool.affine_select(out=heads[:, :, :], in_=heads[:, :, :], compare_op=ALU.is_ge, fill=0.0,
                                   base=HD - 1, pattern=[[-P, 2], [HD, NH]], channel_multiplier=-1).then_inc(sem("heads"), 1)

            @block.tensor
            def _(pe):
                pe.wait_ge(sem("heads"), 3)
                pe.sem_inc(sem("turned"), TPB)
                pe.sem_inc(sem("measured"), 1)

                def step(j, s, lap):
                    if has(j, 1, NB):
                        if has(j, 0, NB):
                            pe.wait_ge(sem("xnt_ready"), j + 1)
                        for u in range(TPB):
                            pe.wait_ge(sem("xn_ready"), j * TPB + (TPB + u + 1))
                            for c in range(DC):
                                last = pe.transpose(psT[:, c, u * P:(u + 1) * P], xn[:, u, c * P:(c + 1) * P], ident[:, :])
                            last.then_inc(sem("turned"), 1)
                    if has(j, 0, NB):
                        pe.wait_ge(sem("xnt_ready"), j + 1)
                        for e in range(NE):
                            if not (isinstance(j, int) and j == 0 and e < 2):
                                pe.wait_ge(sem("q_out"), j * NE + (e - 1))
                            for c in range(DC):
                                last = pe.matmul(psQ[e % 2][:, :], wt[:, c, e * P:(e + 1) * P], xnt[:, s % 2, c, :],
                                                 start=(c == 0), stop=(c == DC - 1))
                            last.then_inc(sem("q_in"), 1)
                        for u in range(TPB):
                            if not (isinstance(j, int) and j == 0 and u < 2):
                                pe.wait_ge(sem("v_out"), j * TPB + (u - 1))
                            for c in range(DC):
                                last = pe.matmul(psV[u % 2][:, :], xnt[:, s % 2, c, u * P:(u + 1) * P], wt[:, c, 2 * D:],
                                                 start=(c == 0), stop=(c == DC - 1))
                            last.then_inc(sem("v_in"), 1)
                        pe.wait_ge(sem("squared"), j * NE + NE)
                        if has(j, -1, NB):
                            pe.wait_ge(sem("norm_out"), j)
                        for n in range(2):
                            for b in range(2):
                                last = pe.matmul(psN[n][:, :], heads[:, b, :], square[:, 2 * n + b, :],
                                                 start=(b == 0), stop=(b == 1))
                        last.then_inc(sem("measured"), 1)

                skewed(pe, NB, 2, step)
                pe.wait_ge(sem("mean_sq"), 1)
                for b in range(2):
                    last = pe.matmul(psN[0][:, 0:1], heads[:, b, :], mean_sq[:, b:b + 1], start=(b == 0), stop=(b == 1))
                last.then_inc(sem("mean_in"), 1)

            @block.scalar
            def _(act):
                act.wait_ge(sem("sqrt"), 1)
                act.activation(tmp[:, :], var[:, :], ACT.Sqrt).then_inc(sem("sqrt"), 1)
                act.wait_ge(sem("bias"), 32)

                def step(j, s, lap):
                    if has(j, 1, NB):
                        act.wait_ge(sem("turned"), j * TPB + 3 * TPB)
                        if has(j, -1, NB):
                            act.wait_ge(sem("v_in"), j * TPB)
                        for c in range(DC):
                            last = act.activation(xnt[:, (s + 1) % 2, c, :], psT[:, c, :], ACT.Copy)
                        last.then_inc(sem("xnt_ready"), 1)
                    if has(j, 0, NB):
                        for e in range(NE):
                            act.wait_ge(sem("q_in"), j * NE + (e + 1))
                            if not (isinstance(j, int) and j == 0 and e < 2):
                                act.wait_ge(sem("split"), j * NE + (e - 1))
                            total = key_sum[:, e - 2, bass.ds(j, 1)] if e >= 2 else None
                            act.activation(full[:, e % 2, :], psQ[e % 2][:, :], ACT.Identity, bias=bias[:, e:e + 1],
                                           accum_out=total)\
                               .then_inc(sem("q_out"), 1)
                            act.wait_ge(sem("q_out"), j * NE + (e + 1))
                            if e == 0:
                                act.wait_ge(sem("measured"), j + 1)
                            act.activation(square[:, e, :], full[:, e % 2, :], ACT.Square).then_inc(sem("squared"), 1)

                skewed(act, NB, 2, step)

            @block.vector
            def _(v):
                own = Chain(v, sem("dve"))
                normalise_stats(v, own.link, X, stats, mean, rstd, tmp, var, sem("stats"), sem("sqrt"))
                v.wait_ge(sem("bias"), 32)

                def step(j, s, lap):
                    if has(j, 1, NB):
                        for u in range(TPB):
                            t = j * TPB + (TPB + u)
                            v.wait_ge(sem("turned"), t + 1)
                            v.tensor_scalar(xn[:, u, :], X[:, t, :], mean[:, bass.ds(t, 1)], rstd[:, bass.ds(t, 1)],
                                            ALU.subtract, ALU.mult).then_inc(sem("xn_ready"), 1)
                    if has(j, 0, NB):
                        for e in range(NE):
                            n = j * NE + e
                            f, r, g = full[:, e % 2, :], rest[:, :], parts[:, e % 2, :, :]
                            v.wait_ge(sem("q_out"), n + 1)
                            v.wait_ge(sem("squared"), n + 1)
                            v.wait_ge(sem(f"part_stored{e % 2}"), (j * (NE // 2) + e // 2) * 16 + 16)
                            if not (isinstance(n, int) and n == 0):
                                v.wait_ge(sem("split"), n)
                            v.tensor_copy(g[:, 0, :], f).then_inc(sem("hi"), 1)
                            v.wait_ge(sem("hi"), n + 1)
                            v.tensor_tensor(r, f, g[:, 0, :], ALU.subtract).then_inc(sem("rest"), 1)
                            v.wait_ge(sem("rest"), n + 1)
                            v.tensor_copy(g[:, 1, :], r).then_inc(sem("mid"), 1)
                            v.wait_ge(sem("mid"), n + 1)
                            v.tensor_tensor(g[:, 2, :], r, g[:, 1, :], ALU.subtract).then_inc(sem("split"), 1)
                        for u in range(TPB):
                            t = j * TPB + u
                            v.wait_ge(sem("v_in"), t + 1)
                            v.tensor_tensor(V[:, t, :], psV[u % 2][:, :], vbias[:, :], ALU.add).then_inc(sem("v_out"), 1)
                        v.wait_ge(sem("measured"), j + 2)
                        v.tensor_scalar(norms[:, bass.ds(j * BLK, BLK)], psN[0][:, :], 1.0, None, ALU.mult)
                        v.tensor_reduce(key_norm[:, bass.ds(j, 1)], psN[1][:, :], AX, ALU.max).then_inc(sem("norm_out"), 1)

                skewed(v, NB, 2, step)
                own.link(v.tensor_reduce(mean_f[:, :], key_sum[:, :, :], AX, ALU.add))
                own.link(v.tensor_scalar(mean_f[:, :], mean_f[:, :], 1.0 / T, None, ALU.mult))
                v.tensor_tensor(mean_sq[:, :], mean_f[:, :], mean_f[:, :], ALU.mult).then_inc(sem("mean_sq"), 1)
                v.wait_ge(sem("mean_in"), 1)
                own.link(v.tensor_copy(key_mean[:, :], psN[0][:, 0:1]))


def bound_shift(nc, sem, sb, pb, ident, norms, key_norm, key_mean, safe, shift_d):
    with ExitStack() as c:
        far = sb("far", [NH, 1], F32, c)
        shift = sb("shift", [NH, T], BF16, c)
        zero = sb("zero_shift", [NH, T], BF16, c)
        worst = sb("worst", [NH, 1], F32, c)
        long = sb("long", [NH, 1], F32, c)
        below = sb("below", [NH, 1], F32, c)
        worst1 = sb("worst1", [1, 1], F32, c)
        psF = pb("psF", [1, NH], F32, c)
        with nc.Block() as block:
            @block.vector
            def _(v):
                own = Chain(v, sem("dve_b"))
                v.memset(zero[:, :], 0.0).then_inc(sem("zeroed"), 1)
                own.link(v.tensor_reduce(far[:, :], key_norm[:, :], AX, ALU.max))
                own.link(v.tensor_reduce(long[:, :], norms[:, :], AX, ALU.max))
                own.link(v.tensor_scalar(long[:, :], long[:, :], key_mean[:, :], 1.1, ALU.mult, ALU.mult))
                v.tensor_scalar(far[:, :], far[:, :], 1.1 / 4, None, ALU.mult).then_inc(sem("far"), 1)
                v.wait_ge(sem("bounded"), 2)
                own.link(v.tensor_reduce(worst[:, :], shift[:, :], AX, ALU.max))
                own.link(v.tensor_tensor(worst[:, :], worst[:, :], below[:, :], ALU.add))
                v.tensor_scalar(shift[:, :], shift[:, :], -1.0, None, ALU.mult).then_inc(sem("negated"), 1)
                v.sem_inc(sem("worst"), 1)
                v.wait_ge(sem("worst_row"), 1)
                own.link(v.tensor_reduce(worst1[:, :], psF[:, :], AX, ALU.max))
                own.link(v.tensor_scalar(safe[:, :], worst1[:, :], LIMIT, None, ALU.is_le))

            @block.scalar
            def _(act):
                act.wait_ge(sem("far"), 1)
                act.activation(shift[:, :], norms[:, :], ACT.Sqrt, scale=far[:, :]).then_inc(sem("bounded"), 1)
                act.activation(below[:, :], long[:, :], ACT.Sqrt).then_inc(sem("bounded"), 1)

            @block.tensor
            def _(pe):
                pe.wait_ge(sem("negated"), 1)
                pe.transpose(psF[:, :], worst[:, :], ident[0:NH, 0:NH]).then_inc(sem("worst_row"), 1)

            @block.sync
            def _(sp):
                sp.wait_ge(sem("zeroed"), 1)
                for n in range(1, NPART):
                    sp.dma_start(shift_d[n], zero[:, :]).then_inc(sem("shift_out"), 16)
                sp.wait_ge(sem("negated"), 1)
                sp.dma_start(shift_d[0], shift[:, :]).then_inc(sem("shift_out"), 16)
                sp.wait_ge(sem("shift_out"), 16 * NPART)


def query_rows(sp, dst, part_d, h, signal):
    row = 0
    for part, times in ((0, 3), (1, 2), (2, 1)):
        for _ in range(times):
            sp.dma_start(dst[row:row + HD, :], part_d[part, bass.ds(h * HD, HD), :]).then_inc(signal, 16)
            row += HD


def key_rows(sp, dst, part_d, h, signal):
    for n, part in enumerate((0, 1, 2, 0, 1, 0)):
        sp.dma_start(dst[n * HD:(n + 1) * HD, :], part_d[part, bass.ds(h * HD + D, HD), :]).then_inc(signal, 16)


def exact_shift(nc, sem, sb, pb, RA, ident, safe, part_d, shift_d):
    ops = RA[:, :].bitcast(BF16).rearrange("p (n t) -> p n t", n=4)
    HALF = T // 2
    with ExitStack() as c:
        half = sb("half_max", [P, NT, 2], F32, c)
        most = sb("most", [P, NT], F32, c)
        neg = sb("neg_most", [NT, P], F32, c)
        rest = sb("neg_rest", [NT, P], F32, c)
        parts = sb("neg_parts", [NT, NPART, P], BF16, c)
        psS = [pb(f"psSx{i}", [P, HALF], F32, c) for i in range(2)]
        with nc.Block() as block:
            @block.sync
            def _(sp):
                ok = sp.value_load(safe[0:1, 0:1], min_val=0, max_val=1)
                with sp.If(ok < 1):
                    with sp.Fori(0, NH) as h:
                        sp.wait_ge(sem("x_free"), h + 1)
                        carried(sp, sem("x_seen_sp"))
                        query_rows(sp, ops[:, 0, :], part_d, h, sem("x_ops"))
                        key_rows(sp, ops[:, 1, :], part_d, h, sem("x_ops"))
                        sp.wait_ge(sem("x_split"), h + 1)
                        carried(sp, sem("x_seen_sp"))
                        sp.dma_start(shift_d[:, bass.ds(h, 1), :].rearrange("a h (t p) -> (h t) a p", p=P), parts[:, :, :])\
                          .then_inc(sem("x_shift"), 16)
                        sp.wait_ge(sem("x_shift"), h * 16 + 16)
                        carried(sp, sem("x_seen_sp"))

            @block.tensor
            def _(pe):
                ok = pe.value_load(safe[0:1, 0:1], min_val=0, max_val=1)
                with pe.If(ok < 1):
                    pe.sem_inc(sem("x_free"), 1)
                    with pe.Fori(0, NH) as h:
                        pe.wait_ge(sem("x_ops"), h * (16 * 12) + 16 * 12)
                        carried(pe, sem("x_seen_pe"))
                        with pe.Fori(0, NT) as t:
                            for n in range(2):
                                pe.wait_ge(sem("x_read"), (h * NT + t) * 2 + (n + 1))
                                for b in range(HALF // BLK):
                                    last = pe.matmul(psS[n][:, b * BLK:(b + 1) * BLK], ops[0:KROWS, 0, bass.ds(t * P, P)],
                                                     ops[0:KROWS, 1, n * HALF + b * BLK:n * HALF + (b + 1) * BLK],
                                                     start=True, stop=True)
                                last.then_inc(sem("x_scores"), 1)
                        pe.wait_ge(sem("x_most"), h + 1)
                        pe.transpose(psS[0][0:NT, 0:P], most[:, :], ident[:, :]).then_inc(sem("x_turned"), 1)
                        pe.sem_inc(sem("x_free"), 1)

            @block.vector
            def _(v):
                ok = v.value_load(safe[0:1, 0:1], min_val=0, max_val=1)
                with v.If(ok < 1):
                    v.sem_inc(sem("x_read"), 2)
                    with v.Fori(0, NH) as h:
                        with v.Fori(0, NT) as t:
                            for n in range(2):
                                k = (h * NT + t) * 2 + n
                                v.wait_ge(sem("x_scores"), k + 1)
                                v.tensor_reduce(half[:, bass.ds(t, 1), n], psS[n][:, :], AX, ALU.max).then_inc(sem("x_read"), 1)
                        v.wait_ge(sem("x_read"), h * (2 * NT) + (2 * NT + 2))
                        v.tensor_tensor(most[:, :], half[:, :, 0], half[:, :, 1], ALU.max).then_inc(sem("x_most"), 1)
                        v.wait_ge(sem("x_turned"), h + 1)
                        v.tensor_scalar(neg[:, :], psS[0][0:NT, 0:P], -1.0, None, ALU.mult).then_inc(sem("x_neg"), 1)
                        v.wait_ge(sem("x_neg"), h * 4 + 1)
                        v.tensor_copy(parts[:, 0, :], neg[:, :]).then_inc(sem("x_neg"), 1)
                        v.wait_ge(sem("x_neg"), h * 4 + 2)
                        v.tensor_tensor(rest[:, :], neg[:, :], parts[:, 0, :], ALU.subtract).then_inc(sem("x_neg"), 1)
                        v.wait_ge(sem("x_neg"), h * 4 + 3)
                        v.tensor_copy(parts[:, 1, :], rest[:, :]).then_inc(sem("x_neg"), 1)
                        v.wait_ge(sem("x_neg"), h * 4 + 4)
                        v.tensor_tensor(parts[:, 2, :], rest[:, :], parts[:, 1, :], ALU.subtract).then_inc(sem("x_split"), 1)
                        v.wait_ge(sem("x_shift"), h * 16 + 16)


def attend(nc, sem, sb, pb, RA, V, part_d, shift_d, head_d):
    ops = RA[:, :].bitcast(BF16).rearrange("p (n t) -> p n t", n=4)
    Q, K = [ops[:, 2 * r, :] for r in range(2)], [ops[:, 2 * r + 1, :] for r in range(2)]
    KT = NT
    QU = T // (4 * BLK)
    W = 2 * BLK
    CH = 4 * BLK // W
    STEPS = 2 * QU * KT
    SLOTS, PS = 3, 4
    CREDIT = 4
    n_chunks = STEPS * CH
    slots = [n % SLOTS for n in range(n_chunks)]
    slots[-4:] = [0, 1, 2, 1]
    LOADS = 13

    def since(n):
        d = 1
        while slots[(n - d) % n_chunks] != slots[n]:
            d += 1
        return d

    with ExitStack() as c:
        values = sb("values", [P, 2, KT, 2 * HD], F32, c)
        probs = sb("probs", [P, PS, W], F32, c)
        sums = sb("sums", [P, 2, BLK], F32, c)
        psS = [pb(f"psS{i}", [P, W], F32, c) for i in range(SLOTS)]
        psO = [pb(f"psO_{i}", [P, BLK], F32, c) for i in range(2)]

        def rounds(eng, body):
            with eng.Fori(0, NH // 2 - 1) as r:
                body(r, False)
            body(NH // 2 - 1, True)

        with nc.Block() as block:
            @block.gpsimd
            def _(pool):
                for r in range(2):
                    pool.memset(values[:, r, :, HD:], 1.0).then_inc(sem("ones"), 1)
                    pool.wait_ge(sem("ones"), 2 * r + 1)
                    pool.memset(K[r][KROWS:QROWS, :], 1.0).then_inc(sem("ones"), 1)
                    pool.wait_ge(sem("ones"), 2 * r + 2)

            @block.sync
            def _(sp):
                def load(h, r):
                    query_rows(sp, Q[r], part_d, h, sem(f"ops{r}"))
                    sp.dma_start(Q[r][KROWS:QROWS, :], shift_d[:, bass.ds(h, 1), :].rearrange("a h t -> (a h) t"))\
                      .then_inc(sem(f"ops{r}"), 16)
                    key_rows(sp, K[r], part_d, h, sem(f"ops{r}"))

                for r in range(2):
                    load(r, r)

                def body(r2, last):
                    for r in range(2):
                        h = r2 * 2 + r
                        for q in range(QU):
                            g = h * QU + q
                            sp.wait_ge(sem("o_out"), g + 3)
                            carried(sp, sem("seen_sp"))
                            for j in range(4):
                                for s in range(2):
                                    sp.dma_start(head_d[4 * q + j, s, bass.ds(h * HD, HD), :],
                                                 sums[32 * j + HD * s:32 * j + HD * (s + 1), q % 2, :])\
                                      .then_inc(sem(f"o_stored{q % 2}"), 16)
                        if not last:
                            sp.wait_ge(sem("pv"), h * (QU * KT) + (QU * KT + 2))
                            carried(sp, sem("seen_sp"))
                            load(h + 2, r)

                rounds(sp, body)
                for q in range(2):
                    sp.wait_ge(sem(f"o_stored{q}"), 16 * 8 * (NH * QU // 2 + 1))

            @block.tensor
            def _(pe):
                pe.wait_ge(sem("ones"), 4)
                pe.sem_inc(sem("pv"), 2)

                def scores(r2, k):
                    r, q, kt = k // (QU * KT), k // KT % QU, k % KT
                    if q == 0 and kt == 0:
                        pe.wait_ge(sem(f"ops{r}"), r2 * (16 * LOADS) + 16 * LOADS)
                    for n in range(CH):
                        m = k * CH + n
                        pe.wait_ge(sem("exped"), r2 * n_chunks + (m - since(m) + 1 + CREDIT))
                        for b in range(W // BLK):
                            at = (q * 4 + n * (W // BLK) + b) * BLK
                            last = pe.matmul(psS[slots[m]][:, b * BLK:(b + 1) * BLK], K[r][0:QROWS, kt * P:(kt + 1) * P],
                                             Q[r][0:QROWS, at:at + BLK], start=True, stop=True)
                        last.then_inc(sem("scored"), 1)

                def weigh(r2, k):
                    r, q, kt = k // (QU * KT), k // KT % QU, k % KT
                    if kt == 0:
                        pe.wait_ge(sem("o_out"), r2 * (2 * QU) + (r * QU + q + 1))
                        if q == 0:
                            pe.wait_ge(sem("filled"), r2 * 2 + (r + 1))
                    pe.wait_ge(sem("exped"), r2 * n_chunks + ((k + 1) * CH + CREDIT))
                    for j in range(4):
                        m = k * CH + j * BLK // W
                        at = j * BLK % W
                        last = pe.matmul(psO[q % 2][32 * j:32 * (j + 1), :], values[:, r, kt, :],
                                         probs[:, m % PS, at:at + BLK], start=(kt == 0), stop=(kt == KT - 1))
                    last.then_inc(sem("pv"), 1)

                def body(r2, last):
                    for k in range(STEPS):
                        if k + 1 < STEPS:
                            scores(r2, k + 1)
                        elif not last:
                            scores(r2 + 1, 0)
                        weigh(r2, k)

                scores(0, 0)
                rounds(pe, body)

            @block.scalar
            def _(act):
                act.sem_inc(sem("exped"), CREDIT)

                def body(r2, last):
                    for m in range(n_chunks):
                        act.wait_ge(sem("scored"), r2 * n_chunks + (m + 1))
                        if m % CH == 0:
                            act.wait_ge(sem("pv"), r2 * STEPS + (m // CH + 1))
                        act.activation(probs[:, m % PS, :], psS[slots[m]][:, :], ACT.Exp, scale=SCALE).then_inc(sem("exped"), 1)

                rounds(act, body)

            @block.vector
            def _(v):
                def fill(h, r):
                    v.tensor_copy(values[:, r, :, 0:HD], V[:, :, bass.ds(h * HD, HD)]).then_inc(sem("filled"), 1)

                for q in range(2):
                    v.sem_inc(sem(f"o_stored{q}"), 16 * 8)
                v.sem_inc(sem("o_out"), 2)
                for r in range(2):
                    fill(r, r)

                def body(r2, last):
                    for r in range(2):
                        h = r2 * 2 + r
                        for q in range(QU):
                            g = h * QU + q
                            v.wait_ge(sem("pv"), g * KT + (KT + 2))
                            v.wait_ge(sem(f"o_stored{q % 2}"), h * (16 * 8) + 16 * 8)
                            v.tensor_copy(sums[:, q % 2, :], psO[q % 2][:, :]).then_inc(sem("o_out"), 1)
                        if not last:
                            fill(h + 2, r)

                rounds(v, body)


def project_out(nc, a, sem, sb, pb, X, pwt, x_d, head_d):
    with ExitStack() as c:
        hd = sb("hd", [P, 2, 2, DC, BLK], F32, c)
        norm = sb("norm", [P, 2, DC, BLK], F32, c)
        pbias = sb("pbias", [P, D], F32, c)
        psP = [pb(f"psP{i}", [P, D], F32, c) for i in range(2)]
        with nc.Block() as block:
            @block.sync
            def _(sp):
                sp.dma_start(pbias[:, :], a["proj_b"].partition_broadcast(P)).then_inc(sem("x_back"), 16)
                sp.dma_start(X, x_d.rearrange("(t p) d -> p t d", p=P)).then_inc(sem("x_back"), 16)
                with sp.Fori(0, NB // 2) as i:
                    for w in range(2):
                        sp.wait_ge(sem("divided"), i * 2 + (w + 1))
                        for s in range(2):
                            sp.dma_start(hd[:, w, s, :, :], head_d[bass.ds(i * 2 + w, 1), s, :, :]
                                         .rearrange("b (c p) q -> p (b c) q", p=P)).then_inc(sem(f"hd{w}"), 16)

            @block.vector
            def _(v):
                v.sem_inc(sem("divided"), 2)
                v.wait_ge(sem("x_back"), 32)
                with v.Fori(0, NB // 2) as i:
                    for w in range(2):
                        b = i * 2 + w
                        v.wait_ge(sem(f"hd{w}"), i * 32 + 32)
                        v.reciprocal(norm[:, w, :, :], hd[:, w, 1, :, :]).then_inc(sem("inverted"), 1)
                        v.wait_ge(sem("inverted"), b + 1)
                        v.tensor_tensor(norm[:, w, :, :], norm[:, w, :, :], hd[:, w, 0, :, :], ALU.mult).then_inc(sem("divided"), 1)
                        for u in range(TPB):
                            t = b * TPB + u
                            v.wait_ge(sem("projected"), t + 1)
                            v.tensor_tensor(X[:, t, :], psP[u % 2][:, :], X[:, t, :], ALU.add).then_inc(sem("p_out"), 1)
                            v.wait_ge(sem("p_out"), t + 3)
                            v.tensor_tensor(X[:, t, :], X[:, t, :], pbias[:, :], ALU.add).then_inc(sem("x_done"), 1)
                v.wait_ge(sem("x_done"), NT)

            @block.tensor
            def _(pe):
                pe.sem_inc(sem("p_out"), 2)
                with pe.Fori(0, NB // 2) as i:
                    for w in range(2):
                        b = i * 2 + w
                        pe.wait_ge(sem("divided"), b + 3)
                        for u in range(TPB):
                            pe.wait_ge(sem("p_out"), b * TPB + (u + 1))
                            for c in range(DC):
                                last = pe.matmul(psP[u % 2][:, :], norm[:, w, c, u * P:(u + 1) * P], pwt[:, c, :],
                                                 start=(c == 0), stop=(c == DC - 1))
                            last.then_inc(sem("projected"), 1)


def ffn_out(nc, a, out, env):
    sem, X = env["sem"], env["X"]
    with nc.Block() as block:
        @block.sync
        def _(sp):
            sp.dma_start(out[0].rearrange("(t p) d -> p t d", p=P), X).then_inc(sem("out"), 16)
            sp.wait_ge(sem("out"), 16)


NAMES = {"x": "L0_attn_x", "qkv_w": "L0_attn_qkv_w", "qkv_b": "L0_attn_qkv_b", "proj_w": "L0_attn_proj_w",
         "proj_b": "L0_attn_proj_b", "Wg": "L0_ffn_Wg", "W1": "L0_ffn_W1", "W2": "L0_ffn_W2", "W3": "L0_ffn_W3",
         "Ws1": "L0_ffn_Ws1", "Ws2": "L0_ffn_Ws2", "Ws3": "L0_ffn_Ws3"}


def kernel(**inputs):
    import concourse.bacc as bacc
    from concourse.bass_utils import run_bass_kernel_spmd

    nc = bacc.Bacc("TRN2", target_bir_lowering=False, num_devices=1)
    arrays, aps = {}, {}
    for short, name in NAMES.items():
        v = np.ascontiguousarray(inputs[name])
        arrays[f"in_{short}"] = v
        aps[short] = nc.dram_tensor(f"in_{short}", v.shape, mybir.dt.from_np(v.dtype), kind="ExternalInput").ap()
    out = nc.dram_tensor("out_x", (1, T, D), F32, kind="ExternalOutput").ap()
    build(nc, aps, out)
    return run_bass_kernel_spmd(nc, [arrays], core_ids=[0]).results[0]["out_x"]
```

```python
import numpy as np
import concourse.bass as bass
from concourse import mybir
from contextlib import ExitStack

F32 = mybir.dt.float32
BF16 = mybir.dt.bfloat16
F16 = mybir.dt.float16
I32 = mybir.dt.int32
ACT = mybir.ActivationFunctionType
ALU = mybir.AluOpType
AX = mybir.AxisListType.X

P = 128
T = 4096
D = 256
DC = D // P
NT = T // P
E = 32
H = 128
HS = 256
HSC = HS // P
TOPK = 4
CAP = 4 * T * TOPK // E
NJ = T * TOPK // P + E
BIG = 32768.0
WCOLS = DC * 2 * H + D
EPS = 1e-5
BLK = 512
NB = T // BLK
TPB = BLK // P
NH = 16
HD = D // NH
SCALE = HD ** -0.5
NPART = 3
KROWS = 6 * HD
QROWS = KROWS + NPART
SAFE = 70.0
LIMIT = SAFE / SCALE


def semaphores(nc, stage, ctx):
    made = {}

    def give_back():
        nc.clear_and_free_semaphores(list(made.values()))
        nc.all_engine_barrier()

    if ctx is not None:
        ctx.callback(give_back)

    def sem(name):
        if name not in made:
            made[name] = nc.alloc_semaphore(f"{stage}_{name}")
        return made[name]

    return sem


class Chain:

    def __init__(self, eng, sem):
        self.eng, self.sem, self.n, self.base = eng, sem, 0, 0

    def mark(self, ins):
        self.n += 1
        ins.then_inc(self.sem, 1)

    def join(self):
        self.eng.wait_ge(self.sem, self.base + self.n)

    def link(self, ins):
        self.mark(ins)
        self.join()


class Loop:

    def __init__(self, chain, i, count, each):
        self.chain, self.count, self.each = chain, count, each
        self.start = chain.n
        chain.base = chain.base + i * each

    def close(self):
        c = self.chain
        assert c.n - self.start == self.each, (c.n - self.start)
        c.base = 0
        c.n = self.start + self.each * self.count


def skewed(eng, count, unroll, step):
    first = 2
    def peeled(j):
        step(j, j % unroll, lambda d: (j + d) // unroll)

    def inside(i, u):
        step(i * unroll + (first + u), (first + u) % unroll, lambda d: i + (first + u + d) // unroll)

    for j in range(-2, first):
        peeled(j)
    rounds = (count - 2 - first) // unroll
    with eng.Fori(0, rounds) as i:
        for u in range(unroll):
            inside(i, u)
    for j in range(first + rounds * unroll, count + 1):
        peeled(j)


def carried(eng, seen):
    eng.sem_inc(seen, 1)


def has(j, d, count):
    return 0 <= j + d < count if isinstance(j, int) else True


def build(nc, a, out):
    ctx = ExitStack()
    with ctx:
        sem = semaphores(nc, "k", None)

        def sb(name, shape, dt, c=ctx):
            return c.enter_context(nc.sbuf_tensor(name, shape, dt))

        def pb(name, shape, dt, c):
            return c.enter_context(nc.psum_tensor(name, shape, dt))

        def dram(name, shape, dt):
            return nc.dram_tensor(name, shape, dt, kind="Internal").ap()

        xn_d = dram("xn_d", (T, D), F32)
        pair_d = dram("pair_d", (NJ * P, D), F32)
        x_d = dram("x_d", (T, D), F32)
        part_d = dram("part_d", (NPART, 2 * D, T), BF16)
        shift_d = dram("shift_d", (NPART, NH, T), BF16)
        head_d = dram("head_d", (NB, 2, D, BLK), F32)

        WE = sb("WE", [P, E, WCOLS], F32)
        RA = sb("RA", [P, NT * D], F32)
        RB = sb("RB", [P, NT * D], F32)
        X = RA[:, :].rearrange("p (t d) -> p t d", t=NT)
        XNT = RB[:, :].rearrange("p (c t) -> p c t", c=DC)
        ident = sb("ident", [P, P], F32)

        with nc.Block() as block:
            @block.sync
            def _(sp):
                for b in range(NB):
                    sp.dma_start(X[:, b * TPB:(b + 1) * TPB, :],
                                 a["x"][0][b * BLK:(b + 1) * BLK, :].rearrange("(t p) d -> p t d", p=P))\
                      .then_inc(sem("x_in"), 16)
                sp.wait_ge(sem("x_in"), 16 * NB)

            @block.gpsimd
            def _(pool):
                pool.memset(ident[:, :], 0.0).then_inc(sem("ident0"), 1)
                pool.wait_ge(sem("ident0"), 1)
                pool.affine_select(out=ident[:, :], in_=ident[:, :], compare_op=ALU.not_equal, fill=1.0,
                                   base=0, pattern=[[-1, P]], channel_multiplier=1).then_inc(sem("ident0"), 1)

        ffn(nc, a, 0, locals())
        attention(nc, a, locals())
        ffn(nc, a, 1, locals())
        ffn_out(nc, a, out, locals())


def normalise_stats(v, link, X, stats, mean, rstd, tmp, var, act_sem, sqrt_sem):
    with v.Fori(0, NT // 4) as i:
        for u in range(4):
            last = v.bn_stats(stats[:, i * 4 + u, :], X[:, i * 4 + u, :])
            last.then_inc(act_sem, 1)
    v.wait_ge(act_sem, NT)
    link(v.tensor_tensor(mean[:, :], stats[:, :, 1], stats[:, :, 4], ALU.add))
    link(v.tensor_tensor(tmp[:, :], stats[:, :, 1], stats[:, :, 4], ALU.subtract))
    link(v.tensor_scalar(mean[:, :], mean[:, :], 0.5, None, ALU.mult))
    link(v.tensor_scalar(tmp[:, :], tmp[:, :], 0.5, None, ALU.mult))
    link(v.tensor_tensor(tmp[:, :], tmp[:, :], tmp[:, :], ALU.mult))
    link(v.tensor_tensor(var[:, :], stats[:, :, 2], stats[:, :, 5], ALU.add))
    link(v.tensor_scalar(var[:, :], var[:, :], 1.0 / D, None, ALU.mult))
    link(v.tensor_tensor(var[:, :], var[:, :], tmp[:, :], ALU.add))
    link(v.tensor_scalar(var[:, :], var[:, :], EPS, None, ALU.add))
    v.sem_inc(sqrt_sem, 1)
    v.wait_ge(sqrt_sem, 2)
    link(v.reciprocal(rstd[:, :], tmp[:, :]))


def ffn(nc, a, L, env):
    sb, pb = env["sb"], env["pb"]
    X, XNT, WE, ident = env["X"], env["XNT"], env["WE"], env["ident"]
    xn_d, pair_d = env["xn_d"], env["pair_d"]

    with ExitStack() as keep:
        sem = semaphores(nc, f"f{L}", keep)
        slot_token = sb(f"slot_token{L}", [P, NJ], I32, keep)
        tile_expert = sb(f"tile_expert{L}", [1, NJ], I32, keep)
        pair_slot = sb(f"pair_slot{L}", [P, NT, TOPK], I32, keep)
        pair_weight = sb(f"pair_weight{L}", [P, NT, TOPK], F32, keep)
        route(nc, a, L, sem, sb, pb, X, XNT, WE, env, ident, xn_d, slot_token, tile_expert, pair_slot, pair_weight)
        experts(nc, L, sem, sb, pb, WE, ident, xn_d, pair_d, slot_token, tile_expert, env)
        combine(nc, a, L, sem, sb, pb, X, XNT, pair_d, pair_slot, pair_weight, env)


def route(nc, a, L, sem, sb, pb, X, XNT, WE, env, ident, xn_d, slot_token, tile_expert, pair_slot, pair_weight):
    U = 4
    with ExitStack() as c:
        stats = sb(f"stats{L}", [P, NT, 6], F32, c)
        mean = sb(f"mean{L}", [P, NT], F32, c)
        rstd = sb(f"rstd{L}", [P, NT], F32, c)
        var = sb(f"var{L}", [P, NT], F32, c)
        tmp = sb(f"tmp{L}", [P, NT], F32, c)
        wg = sb(f"wg{L}", [P, DC, E], F32, c)
        xn = sb(f"xn{L}", [P, U, D], F32, c)
        SC = sb(f"SC{L}", [P, NT, E], F32, c)
        A1 = sb(f"A1{L}", [P, NT, E], F32, c)
        A2 = sb(f"A2{L}", [P, NT, E], F32, c)
        TW = sb(f"TW{L}", [P, NT, E], F32, c)
        M = sb(f"M{L}", [P, NT, E], BF16, c)
        R = sb(f"R{L}", [P, NT + 1, E], BF16, c)
        top8 = sb(f"top8{L}", [P, NT, 8], F32, c)
        slot8 = sb(f"slot8{L}", [P, NT, 8], F32, c)
        row1 = sb(f"row1{L}", [P, NT], F32, c)
        row2 = sb(f"row2{L}", [P, NT], F32, c)
        base = sb(f"base{L}", [P, E], F32, c)
        earlier = sb(f"earlier{L}", [P, P], BF16, c)
        upto = sb(f"upto{L}", [E, 2 * E], BF16, c)
        ones = sb(f"ones{L}", [P, P], BF16, c)
        zeros = sb(f"zeros{L}", [P, P], F16, c)
        zrow = sb(f"zrow{L}", [P, NJ], F16, c)
        cnt_f = sb(f"cnt_f{L}", [E, 1], F32, c)
        cnt_i = sb(f"cnt_i{L}", [E, 1], I32, c)
        tiles_bf = sb(f"tiles_bf{L}", [E, 1], BF16, c)
        tiles_f = sb(f"tiles_f{L}", [E, 1], F32, c)
        spread = sb(f"spread{L}", [E, 2 * E], BF16, c)
        end_col = sb(f"end_col{L}", [E, 1], F32, c)
        past = sb(f"past{L}", [E, NJ], BF16, c)
        iota_i = sb(f"iota_i{L}", [P, NJ], I32, c)
        iota_h = sb(f"iota_h{L}", [P, NJ], F16, c)
        iota_f = sb(f"iota_f{L}", [P, NJ], F32, c)
        number_i = sb(f"number_i{L}", [P, NT], I32, c)
        number = sb(f"number{L}", [P, NT], F32, c)
        pf = sb(f"pf{L}", [P, NT, TOPK], F32, c)
        pv = sb(f"pv{L}", [P, NT, TOPK], F32, c)
        pi = sb(f"pi{L}", [P, NT, TOPK], I32, c)
        lo_f = sb(f"lo_f{L}", [P, NT, TOPK], F32, c)
        lo_now = sb(f"lo_now{L}", [P, 2, TOPK // 2], F32, c)
        hi_f = sb(f"hi_f{L}", [P, NT, TOPK], F32, c)
        at_row = sb(f"at_row{L}", [P, 2 * TOPK, P], F16, c)
        at_tile = sb(f"at_tile{L}", [P, 2 * TOPK, NJ], F16, c)
        tok_f = sb(f"tok_f{L}", [P, NJ], F32, c)
        psT = [pb(f"psT{i}_{L}", [P, DC * P], F32, c) for i in range(2)]
        psL = pb(f"psL{L}", [P, NT * E], F32, c)
        psR = pb(f"psR{L}", [P, NT * E], F32, c)
        psI = pb(f"psI{L}", [P, 512], F32, c)
        psM = pb(f"psM{L}", [P, 512], F32, c)

        def by_tile(ap):
            return ap.rearrange("p (t e) -> p t e", e=E)

        def over_experts(ap):
            return ap.unsqueeze(2).to_broadcast([P, NT, E])

        with nc.Block() as block:
            @block.sync
            def _(sp):
                sp.dma_start(wg[:, :, :], a["Wg"].rearrange("(c p) e -> p c e", p=P)).then_inc(sem("wg"), 16)
                for u in range(U):
                    sp.sem_inc(sem(f"xn_stored{u}"), 16)
                with sp.Fori(0, NT // U) as i:
                    for u in range(U):
                        t = i * U + u
                        sp.wait_ge(sem("xn_ready"), t + 1)
                        sp.dma_start(xn_d[bass.ds(t * P, P), :], xn[:, u, :]).then_inc(sem(f"xn_stored{u}"), 16)
                for u in range(U):
                    sp.wait_ge(sem(f"xn_stored{u}"), 16 * (1 + NT // U))

            @block.gpsimd
            def _(pool):
                own = Chain(pool, sem("pool"))
                pool.memset(ones[:, :], 1.0)
                pool.memset(zeros[:, :], 0.0)
                pool.memset(zrow[:, :], 0.0)
                pool.memset(earlier[:, :], 1.0).then_inc(sem("consts"), 1)
                pool.memset(upto[:, :], 1.0).then_inc(sem("consts"), 1)
                pool.memset(R[:, 0, :], 0.0).then_inc(sem("consts"), 1)
                pool.wait_ge(sem("consts"), 3)
                pool.affine_select(out=earlier[:, :], in_=earlier[:, :], compare_op=ALU.is_gt, fill=0.0,
                                   base=0, pattern=[[1, P]], channel_multiplier=-1).then_inc(sem("consts"), 1)
                pool.affine_select(out=upto[:, 0:E], in_=upto[:, 0:E], compare_op=ALU.is_ge, fill=0.0,
                                   base=0, pattern=[[1, E]], channel_multiplier=-1).then_inc(sem("consts"), 1)
                pool.affine_select(out=upto[:, E:2 * E], in_=upto[:, E:2 * E], compare_op=ALU.is_gt, fill=0.0,
                                   base=0, pattern=[[1, E]], channel_multiplier=-1).then_inc(sem("consts"), 1)
                pool.iota(iota_i[:, :], pattern=[[1, NJ]], base=0, channel_multiplier=0).then_inc(sem("consts"), 1)
                pool.iota(number_i[:, :], pattern=[[P, NT]], base=-T // 2, channel_multiplier=1).then_inc(sem("consts"), 1)
                pool.wait_ge(sem("lo_ready"), 1)
                pool.sem_inc(sem("row_onehot"), 1)
                with pool.Fori(0, NT // 2) as i:
                    pool.wait_ge(sem("row_onehot"), i * TOPK + 1)
                    pool.tensor_copy(lo_now[:, :, :], lo_f[:, bass.ds(i * 2, 2), 0:TOPK // 2]).then_inc(sem("row_fetched"), 1)
                    pool.wait_ge(sem("row_fetched"), i + 1)
                    for w in range(2):
                        pool.wait_ge(sem("placed"), i * (2 * TOPK) + (w * TOPK + TOPK // 2))
                        carried(pool, sem("seen_row"))
                        for k in range(TOPK // 2):
                            pool.tensor_scalar(at_row[:, w * TOPK + k, :], iota_h[:, 0:P], lo_now[:, w, k:k + 1], None,
                                               ALU.is_equal).then_inc(sem("row_onehot"), 1)

            @block.scalar
            def _(act):
                act.wait_ge(sem("sqrt"), 1)
                act.activation(tmp[:, :], var[:, :], ACT.Sqrt).then_inc(sem("sqrt"), 1)
                with act.Fori(0, NT // U) as i:
                    for u in range(U):
                        t = i * U + u
                        act.wait_ge(sem("turned"), t + 1 + U)
                        act.activation(XNT[:, :, bass.ds(t * P, P)], psT[u % 2][:, :].rearrange("p (c t) -> p c t", c=DC), ACT.Copy)\
                           .then_inc(sem("xnt_ready"), 1)
                if L == 0:
                    for c in range(DC):
                        for n, w in enumerate(("W1", "W3")):
                            act.dma_start(WE[:, :, (2 * c + n) * H:(2 * c + n + 1) * H],
                                          a[w][:, c * P:(c + 1) * P, :].rearrange("e p h -> p e h"))\
                               .then_inc(env["sem"]("we_in"), 16)
                    act.dma_start(WE[:, :, DC * 2 * H:], a["W2"].rearrange("e h d -> h e d")).then_inc(env["sem"]("we_in"), 16)
                act.wait_ge(sem("shifted"), 1)
                act.activation(SC[:, :, :], SC[:, :, :], ACT.Exp).then_inc(sem("exped"), 1)

            @block.tensor
            def _(pe):
                pe.wait_ge(sem("wg"), 16)
                pe.sem_inc(sem("turned"), U)

                def turn(t, u):
                    pe.wait_ge(sem("xn_ready"), t + 1)
                    if t >= 2:
                        pe.wait_ge(sem("xnt_ready"), t - 1)
                    for c in range(DC):
                        last = pe.transpose(psT[u % 2][:, c * P:(c + 1) * P], xn[:, u, c * P:(c + 1) * P], ident[:, :])
                    last.then_inc(sem("turned"), 1)

                def logits(t):
                    pe.wait_ge(sem("xnt_ready"), t + 1)
                    for c in range(DC):
                        last = pe.matmul(psL[:, t * E:(t + 1) * E], XNT[:, c, t * P:(t + 1) * P], wg[:, c, :],
                                         start=(c == 0), stop=(c == DC - 1))
                    last.then_inc(sem("routed"), 1)

                for t in range(NT):
                    turn(t, t % U)
                    if t:
                        logits(t - 1)
                logits(NT - 1)

                pe.wait_ge(sem("masked"), 1)
                Mf, Rf = M[:, :, :].rearrange("p t e -> p (t e)"), R[:, 0:NT, :].rearrange("p t e -> p (t e)")
                for b in range(NT * E // 512):
                    w = slice(b * 512, (b + 1) * 512)
                    pe.matmul(psR[:, w], earlier[:, :], Mf[:, w], start=True, stop=False)
                    pe.matmul(psR[:, w], ones[:, :], Rf[:, w], start=False, stop=True)
                pe.matmul(psM[0:E, 0:1], R[:, NT, :], ones[:, 0:1], start=True, stop=True).then_inc(sem("ranked"), 1)
                pe.wait_ge(sem("sized"), 1)
                pe.matmul(psM[:, 64:128], ones[0:E, :], spread[:, :], start=True, stop=True)
                pe.matmul(psM[0:E, 1:2], upto[:, 0:E], tiles_bf[:, :], start=True, stop=True).then_inc(sem("ends"), 1)
                pe.wait_ge(sem("past"), 1)
                pe.matmul(psM[0:1, 128:128 + NJ], ones[0:E, 0:1], past[:, :], start=True, stop=True).then_inc(sem("owners"), 1)
                pe.matmul(psI[:, 0:NJ], zeros[:, :], zrow[:, :], start=True, stop=False)
                pe.sem_inc(sem("placed"), 2 * TOPK)
                with pe.Fori(0, NT // 2) as i:
                    for w in range(2):
                        for k in range(TOPK):
                            b = w * TOPK + k
                            pe.wait_ge(sem("onehot"), i * (2 * TOPK) + (b + 1))
                            if k < TOPK // 2:
                                pe.wait_ge(sem("row_onehot"), i * TOPK + (w * (TOPK // 2) + k + 2))
                            pe.matmul(psI[:, 0:NJ], at_row[:, b, :], at_tile[:, b, :],
                                      start=False, stop=False, skip_group_check=True).then_inc(sem("placed"), 1)
                pe.matmul(psI[:, 0:NJ], zeros[:, :], zrow[:, :], start=False, stop=True).then_inc(sem("all_placed"), 1)

            @block.vector
            def _(v):
                own = Chain(v, sem("dve"))
                link, mark, join = own.link, own.mark, own.join
                normalise_stats(v, link, X, stats, mean, rstd, tmp, var, sem("stats"), sem("sqrt"))
                with v.Fori(0, NT // U) as i:
                    for u in range(U):
                        t = i * U + u
                        v.wait_ge(sem("turned"), t + 1)
                        v.wait_ge(sem(f"xn_stored{u}"), i * 16 + 16)
                        v.tensor_scalar(xn[:, u, :], X[:, t, :], mean[:, bass.ds(t, 1)], rstd[:, bass.ds(t, 1)],
                                        ALU.subtract, ALU.mult).then_inc(sem("xn_ready"), 1)
                v.wait_ge(sem("consts"), 8)
                mark(v.tensor_copy(iota_f[:, :], iota_i[:, :]))
                mark(v.tensor_copy(iota_h[:, :], iota_i[:, :]))
                mark(v.tensor_copy(number[:, :], number_i[:, :]))

                v.wait_ge(sem("routed"), NT)
                link(v.tensor_reduce(row1[:, :], by_tile(psL[:, :]), AX, ALU.max))
                v.tensor_tensor(SC[:, :, :], by_tile(psL[:, :]), over_experts(row1[:, :]), ALU.subtract)\
                 .then_inc(sem("shifted"), 1)
                v.wait_ge(sem("exped"), 1)
                link(v.tensor_reduce(row2[:, :], SC[:, :, :], AX, ALU.add))
                link(v.reciprocal(row2[:, :], row2[:, :]))
                link(v.tensor_tensor(SC[:, :, :], SC[:, :, :], over_experts(row2[:, :]), ALU.mult))

                for t in range(NT):
                    mark(v.max(top8[:, t, :], SC[:, t, :]))
                join()
                link(v.memset(top8[:, :, TOPK:], -1.0))
                for t in range(NT):
                    mark(v.match_replace(A1[:, t, :], top8[:, t, :], SC[:, t, :], -2.0))
                join()
                link(v.tensor_scalar(M[:, :, :], A1[:, :, :], -1.5, None, ALU.is_lt))
                for t in range(NT):
                    last = v.tensor_tensor(R[:, t + 1, :], R[:, t, :], M[:, t, :], ALU.add)
                    if t < NT - 1:
                        link(last)
                last.then_inc(sem("masked"), 1)

                v.wait_ge(sem("ranked"), 1)
                link(v.tensor_scalar(cnt_f[:, :], psM[0:E, 0:1], float(CAP), float(P - 1), ALU.min, ALU.add))
                link(v.tensor_copy(cnt_i[:, :], cnt_f[:, :]))
                link(v.tensor_scalar(cnt_i[:, :], cnt_i[:, :], 7, None, ALU.arith_shift_right))
                link(v.tensor_copy(tiles_f[:, :], cnt_i[:, :]))
                mark(v.tensor_copy(tiles_bf[:, :], tiles_f[:, :]))
                join()
                v.tensor_scalar(spread[:, :], upto[:, :], tiles_f[:, :], None, ALU.mult).then_inc(sem("sized"), 1)
                v.wait_ge(sem("ends"), 1)
                link(v.tensor_copy(end_col[:, :], psM[0:E, 1:2]))
                link(v.tensor_scalar(base[:, :], psM[:, 64 + E:64 + 2 * E], float(P), None, ALU.mult))
                v.tensor_scalar(past[:, :], iota_f[0:E, :], end_col[:, :], None, ALU.is_ge).then_inc(sem("past"), 1)

                link(v.tensor_scalar(A1[:, :, :], by_tile(psR[:, :]), float(CAP), None, ALU.is_lt))
                link(v.tensor_tensor(A1[:, :, :], A1[:, :, :], M[:, :, :], ALU.mult))
                mark(v.tensor_tensor(TW[:, :, :], SC[:, :, :], A1[:, :, :], ALU.mult))
                link(v.tensor_tensor(A2[:, :, :], by_tile(psR[:, :]), base[:, :].unsqueeze(1).to_broadcast([P, NT, E]), ALU.add))
                link(v.tensor_scalar(A2[:, :, :], A2[:, :, :], -1.0, BIG, ALU.mult, ALU.add))
                link(v.tensor_tensor(A2[:, :, :], A2[:, :, :], A1[:, :, :], ALU.mult))
                for t in range(NT):
                    mark(v.max(slot8[:, t, :], A2[:, t, :]))
                join()
                link(v.tensor_scalar(pv[:, :, :], slot8[:, :, 0:TOPK], 0.0, None, ALU.is_gt))
                link(v.tensor_scalar(pf[:, :, :], slot8[:, :, 0:TOPK], -1.0, BIG, ALU.mult, ALU.add))
                link(v.tensor_tensor(pf[:, :, :], pf[:, :, :], pv[:, :, :], ALU.mult))
                link(v.tensor_copy(pair_slot[:, :, :], pf[:, :, :]))
                link(v.tensor_scalar(pi[:, :, :], pair_slot[:, :, :], P - 1, None, ALU.bitwise_and))
                link(v.tensor_copy(lo_f[:, :, :], pi[:, :, :]))
                link(v.tensor_scalar(pi[:, :, :], pair_slot[:, :, :], 7, None, ALU.arith_shift_right))
                link(v.tensor_copy(hi_f[:, :, :], pi[:, :, :]))
                link(v.tensor_scalar(pv[:, :, :], pv[:, :, :], -1000.0, 1000.0, ALU.mult, ALU.add))
                link(v.tensor_tensor(hi_f[:, :, :], hi_f[:, :, :], pv[:, :, :], ALU.add))

                v.sem_inc(sem("lo_ready"), 1)

                with v.Fori(0, NT // 2) as i:
                    for w in range(2):
                        for k in range(TOPK):
                            t, b = i * 2 + w, w * TOPK + k
                            v.wait_ge(sem("placed"), i * (2 * TOPK) + (b + 1))
                            if k >= TOPK // 2:
                                v.tensor_scalar(at_row[:, b, :], iota_h[:, 0:P], lo_f[:, bass.ds(t, 1), k], None, ALU.is_equal)
                            v.tensor_scalar(at_tile[:, b, :], iota_h[:, :], hi_f[:, bass.ds(t, 1), k], number[:, bass.ds(t, 1)],
                                            ALU.is_equal, ALU.mult).then_inc(sem("onehot"), 1)

                for k in range(TOPK):
                    link(v.tensor_tensor(A1[:, :, :], A2[:, :, :], over_experts(slot8[:, :, k]), ALU.is_equal))
                    link(v.tensor_tensor(A1[:, :, :], A1[:, :, :], TW[:, :, :], ALU.mult))
                    link(v.tensor_reduce(pair_weight[:, :, k], A1[:, :, :], AX, ALU.add))
                link(v.tensor_scalar(pair_weight[:, :, :], pair_weight[:, :, :], 0.5, None, ALU.mult))
                v.wait_ge(sem("owners"), 1)
                link(v.tensor_scalar(tile_expert[:, :], psM[0:1, 128:128 + NJ], float(E - 1), None, ALU.min))
                v.wait_ge(sem("all_placed"), 1)
                link(v.tensor_scalar(tok_f[:, :], psI[:, 0:NJ], float(T // 2), None, ALU.add))
                link(v.tensor_copy(slot_token[:, :], tok_f[:, :]))


def experts(nc, L, sem, sb, pb, WE, ident, xn_d, pair_d, slot_token, tile_expert, env):
    U = 4
    gathered = [env["sem"](f"gathered{u}") for u in range(U)]
    with ExitStack() as c:
        index = sb(f"index{L}", [P, U], I32, c)
        xg = sb(f"xg{L}", [P, U, D], F32, c)
        xgt = sb(f"xgt{L}", [P, 2, D], F32, c)
        gate = sb(f"gate{L}", [P, 2, H], F32, c)
        hid = sb(f"hid{L}", [P, 2, H], F32, c)
        hidt = sb(f"hidt{L}", [P, 2, H], F32, c)
        ob = sb(f"ob{L}", [P, U, D], F32, c)
        psX = [pb(f"psX{i}_{L}", [P, D], F32, c) for i in range(2)]
        psH = [pb(f"psH{i}_{L}", [P, 2 * H], F32, c) for i in range(2)]
        psG = [pb(f"psG{i}_{L}", [P, H], F32, c) for i in range(2)]
        psO = [pb(f"psO{i}_{L}", [P, D], F32, c) for i in range(2)]

        with nc.Block() as block:
            @block.gpsimd
            def _(pool):
                with pool.Fori(0, NJ // U) as i:
                    for u in range(U):
                        j = i * U + u
                        pool.wait_ge(sem("x_turned"), j + 1)
                        pool.tensor_copy(index[:, u:u + 1], slot_token[:, bass.ds(j, 1)]).then_inc(sem("indexed"), 1)
                        pool.wait_ge(sem("indexed"), j + 1)
                        pool.sem_inc(sem("index_seen"), 1)
                        pool.indirect_dma_start(xg[:, u, :], None, xn_d, bass.IndirectOffsetOnAxis(ap=index[:, u:u + 1], axis=0))\
                            .then_inc(gathered[u], 16)

            @block.tensor
            def _(pe):
                if L == 0:
                    pe.wait_ge(env["sem"]("we_in"), 16 * 5)
                pe.sem_inc(sem("x_turned"), U)
                owner = [pe.alloc_register(f"owner{u}_{L}") for u in range(U)]

                def step(j, s, lap):
                    if has(j, 2, NJ):
                        pe.wait_ge(gathered[(s + 2) % U], lap(2) * 16 + (16 + L * 16 * NJ // U))
                        if has(j, 0, NJ):
                            pe.wait_ge(sem("xgt_ready"), j + 1)
                        for c in range(DC):
                            last = pe.transpose(psX[s % 2][:, c * P:(c + 1) * P], xg[:, (s + 2) % U, c * P:(c + 1) * P], ident[:, :])
                        last.then_inc(sem("x_turned"), 1)
                    if has(j, 1, NJ):
                        e = pe.snap(owner[(s + 1) % U], min_val=0, max_val=E - 1)
                        pe.wait_ge(sem("xgt_ready"), j + 2)
                        if has(j, -1, NJ):
                            pe.wait_ge(sem("hid_ready"), j)
                        for c in range(DC):
                            last = pe.matmul(psH[(s + 1) % 2][:, :], xgt[:, (s + 1) % 2, c * P:(c + 1) * P],
                                             WE[:, e, c * 2 * H:(c + 1) * 2 * H], start=(c == 0), stop=(c == DC - 1))
                        last.then_inc(sem("up"), 1)
                    if has(j, 2, NJ):
                        pe.reg_load(owner[(s + 2) % U], tile_expert[0:1, bass.ds(j + 2, 1)])
                    if has(j, 0, NJ):
                        pe.wait_ge(sem("hid_ready"), j + 1)
                        if has(j, -2, NJ):
                            pe.wait_ge(sem("hidt_ready"), j - 1)
                        pe.transpose(psG[s % 2][:, :], hid[:, s % 2, :], ident[:, :]).then_inc(sem("h_turned"), 1)
                    if has(j, -1, NJ):
                        e = pe.snap(owner[(s - 1) % U], min_val=0, max_val=E - 1)
                        pe.wait_ge(sem("hidt_ready"), j)
                        if has(j, -3, NJ):
                            pe.wait_ge(sem("ob_ready"), j - 2)
                        pe.matmul(psO[(s - 1) % 2][:, :], hidt[:, (s - 1) % 2, :], WE[:, e, DC * 2 * H:],
                                  start=True, stop=True).then_inc(sem("down"), 1)

                skewed(pe, NJ, U, step)

            @block.vector
            def _(v):
                def step(j, s, lap):
                    if has(j, 2, NJ):
                        v.wait_ge(sem("x_turned"), j + 3 + U)
                        if has(j, 0, NJ):
                            v.wait_ge(sem("up"), j + 1)
                        v.tensor_copy(xgt[:, s % 2, :], psX[s % 2][:, :]).then_inc(sem("xgt_ready"), 1)
                    if has(j, 1, NJ):
                        v.wait_ge(sem("gated"), j + 2)
                        if has(j, -1, NJ):
                            v.wait_ge(sem("h_turned"), j)
                        v.tensor_tensor(hid[:, (s + 1) % 2, :], gate[:, (s + 1) % 2, :], psH[(s + 1) % 2][:, H:], ALU.mult)\
                         .then_inc(sem("hid_ready"), 1)

                skewed(v, NJ, U, step)

            @block.scalar
            def _(act):
                for u in range(U):
                    act.sem_inc(sem(f"stored{u}"), 16)

                def step(j, s, lap):
                    if has(j, 1, NJ):
                        act.wait_ge(sem("up"), j + 2)
                        if has(j, -1, NJ):
                            act.wait_ge(sem("hid_ready"), j)
                        act.activation(gate[:, (s + 1) % 2, :], psH[(s + 1) % 2][:, 0:H], ACT.Silu).then_inc(sem("gated"), 1)
                    if has(j, 0, NJ):
                        act.wait_ge(sem("h_turned"), j + 1)
                        if has(j, -2, NJ):
                            act.wait_ge(sem("down"), j - 1)
                        act.activation(hidt[:, s % 2, :], psG[s % 2][:, :], ACT.Copy).then_inc(sem("hidt_ready"), 1)
                    if has(j, -1, NJ):
                        act.wait_ge(sem("down"), j)
                        act.wait_ge(sem(f"stored{(s - 1) % U}"), lap(-1) * 16 + 16)
                        act.activation(ob[:, (s - 1) % U, :], psO[(s - 1) % 2][:, :], ACT.Copy).then_inc(sem("ob_ready"), 1)

                skewed(act, NJ, U, step)

            @block.sync
            def _(sp):
                with sp.Fori(0, NJ // U) as i:
                    for u in range(U):
                        j = i * U + u
                        sp.wait_ge(sem("ob_ready"), j + 1)
                        sp.dma_start(pair_d[bass.ds(j * P, P), :], ob[:, u, :]).then_inc(sem(f"stored{u}"), 16)
                for u in range(U):
                    sp.wait_ge(sem(f"stored{u}"), 16 * (1 + NJ // U))


def combine(nc, a, L, sem, sb, pb, X, XNT, pair_d, pair_slot, pair_weight, env):
    YS = 2 * TOPK
    y_in = [env["sem"](f"y_in{s}") for s in range(YS)]
    with ExitStack() as c:
        ws1 = sb(f"ws1{L}", [P, DC, HS], F32, c)
        ws3 = sb(f"ws3{L}", [P, DC, HS], F32, c)
        ws2 = sb(f"ws2{L}", [P, HSC, D], F32, c)
        index = sb(f"cindex{L}", [P, 2, 2, TOPK], I32, c)
        Y = sb(f"Y{L}", [P, YS, D], F32, c)
        gate = sb(f"sgate{L}", [P, HSC, BLK], F32, c)
        hid = sb(f"shid{L}", [P, HSC, BLK], F32, c)
        psA = [pb(f"psA{i}_{L}", [P, BLK], F32, c) for i in range(HSC)]
        psB = [pb(f"psB{i}_{L}", [P, BLK], F32, c) for i in range(HSC)]
        psZ = [pb(f"psZ{i}_{L}", [P, D], F32, c) for i in range(2)]

        with nc.Block() as block:
            @block.sync
            def _(sp):
                sp.dma_start(ws1[:, :, :], a["Ws1"].rearrange("(c p) h -> p c h", p=P)).then_inc(sem("ws"), 16)
                sp.dma_start(ws3[:, :, :], a["Ws3"].rearrange("(c p) h -> p c h", p=P)).then_inc(sem("ws"), 16)
                sp.dma_start(ws2[:, :, :], a["Ws2"].rearrange("(c p) d -> p c d", p=P)).then_inc(sem("ws"), 16)

            @block.gpsimd
            def _(pool):
                pool.sem_inc(sem("y_used"), YS)
                with pool.Fori(0, NT // 4) as i:
                    for w in range(2):
                        pool.tensor_copy(index[:, w, :, :], pair_slot[:, bass.ds(i * 4 + 2 * w, 2), :]).then_inc(sem("y_indexed"), 1)
                        pool.wait_ge(sem("y_indexed"), i * 2 + (w + 1))
                        for u in range(2):
                            pool.wait_ge(sem("y_used"), i * (4 * TOPK) + (2 * w + u + 1) * TOPK)
                            carried(pool, sem("seen_pool"))
                            for k in range(TOPK):
                                s = u * TOPK + k
                                pool.indirect_dma_start(Y[:, s, :], None, pair_d,
                                                        bass.IndirectOffsetOnAxis(ap=index[:, w, u, k:k + 1], axis=0))\
                                    .then_inc(y_in[s], 16)

            @block.tensor
            def _(pe):
                pe.wait_ge(sem("ws"), 48)
                pe.sem_inc(sem("z_added"), 2)
                pe.sem_inc(sem("s_hid"), HSC)
                with pe.Fori(0, NB) as b:
                    for m in range(HSC):
                        pe.wait_ge(sem("s_hid"), b * HSC + (m + 1))
                        for ps, w in ((psA, ws1), (psB, ws3)):
                            for c in range(DC):
                                last = pe.matmul(ps[m][:, :], w[:, c, m * P:(m + 1) * P], XNT[:, c, bass.ds(b * BLK, BLK)],
                                                 start=(c == 0), stop=(c == DC - 1))
                        last.then_inc(sem("s_up"), 1)
                    for u in range(TPB):
                        t = b * TPB + u
                        if u == 0:
                            pe.wait_ge(sem("s_hid"), b * HSC + 2 * HSC)
                        pe.wait_ge(sem("z_added"), t + 1)
                        for m in range(HSC):
                            last = pe.matmul(psZ[u % 2][:, :], hid[:, m, u * P:(u + 1) * P], ws2[:, m, :],
                                             start=(m == 0), stop=(m == HSC - 1))
                        last.then_inc(sem("z_ready"), 1)

            @block.scalar
            def _(act):
                with act.Fori(0, NB) as b:
                    for m in range(HSC):
                        act.wait_ge(sem("s_up"), b * HSC + (m + 1))
                        act.wait_ge(sem("s_hid"), b * HSC + (m + 1))
                        act.activation(gate[:, m, :], psA[m][:, :], ACT.Silu).then_inc(sem("s_gate"), 1)

            @block.vector
            def _(v):
                with v.Fori(0, NB) as b:
                    for m in range(HSC):
                        v.wait_ge(sem("s_gate"), b * HSC + (m + 1))
                        v.tensor_tensor(hid[:, m, :], gate[:, m, :], psB[m][:, :], ALU.mult).then_inc(sem("s_hid"), 1)
                    for u in range(TPB):
                        t = b * TPB + u
                        v.wait_ge(sem("z_ready"), t + 1)
                        v.scalar_tensor_tensor(X[:, t, :], psZ[u % 2][:, :], 0.5, X[:, t, :], ALU.mult, ALU.add)\
                         .then_inc(sem("z_added"), 1)
                        v.wait_ge(sem("z_added"), t + 3)
                        for k in range(TOPK):
                            n = t * TOPK + k
                            v.wait_ge(y_in[(u % 2) * TOPK + k], (b * (TPB // 2) + u // 2) * 16 + (16 + L * 16 * NT // 2))
                            v.scalar_tensor_tensor(X[:, t, :], Y[:, (u % 2) * TOPK + k, :], pair_weight[:, bass.ds(t, 1), k],
                                                   X[:, t, :], ALU.mult, ALU.add).then_inc(sem("y_used"), 1)
                            v.wait_ge(sem("y_used"), n + (YS + 1))


def attention(nc, a, env):
    sb, pb = env["sb"], env["pb"]
    X, RA, RB, ident = env["X"], env["RA"], env["RB"], env["ident"]
    x_d, part_d, shift_d, head_d = env["x_d"], env["part_d"], env["shift_d"], env["head_d"]
    V = RB[:, :].rearrange("p (t d) -> p t d", t=NT)

    with ExitStack() as c:
        sem = semaphores(nc, "a", c)
        pwt = sb("pwt", [P, DC, D], F32, c)
        norms = sb("norms", [NH, T], BF16, c)
        key_norm = sb("key_norm", [NH, NB], F32, c)
        key_mean = sb("key_mean", [NH, 1], F32, c)
        safe = sb("safe", [1, 1], I32, c)
        with ExitStack() as c2:
            wt = sb("wt", [P, DC, 3 * D], F32, c2)
            project_heads(nc, a, sem, sb, pb, X, V, RB, ident, wt, pwt, norms, key_norm, key_mean, x_d, part_d)
        bound_shift(nc, sem, sb, pb, ident, norms, key_norm, key_mean, safe, shift_d)
        exact_shift(nc, sem, sb, pb, RA, ident, safe, part_d, shift_d)
        attend(nc, sem, sb, pb, RA, V, part_d, shift_d, head_d)
        project_out(nc, a, sem, sb, pb, X, pwt, x_d, head_d)


def project_heads(nc, a, sem, sb, pb, X, V, RB, ident, wt, pwt, norms, key_norm, key_mean, x_d, part_d):
    NE = 2 * D // P
    NQ, NW = 3 * D // P, 4 * D // P
    raw = RB[:, 0:NW * D].rearrange("p (b d) -> p b d", d=D)
    with ExitStack() as c:
        stats = sb("astats", [P, NT, 6], F32, c)
        mean = sb("amean", [P, NT], F32, c)
        rstd = sb("arstd", [P, NT], F32, c)
        var = sb("avar", [P, NT], F32, c)
        tmp = sb("atmp", [P, NT], F32, c)
        xn = sb("axn", [P, TPB, D], F32, c)
        xnt = sb("axnt", [P, 2, DC, BLK], F32, c)
        full = sb("full", [P, 2, BLK], F32, c)
        rest = sb("rest", [P, BLK], F32, c)
        parts = sb("parts", [P, 2, NPART, BLK], BF16, c)
        square = sb("square", [P, NE, BLK], BF16, c)
        bias = sb("bias", [P, NE], F32, c)
        vbias = sb("vbias", [P, D], F32, c)
        heads = sb("heads", [P, 2, NH], BF16, c)
        key_sum = sb("key_sum", [P, 2, NB], F32, c)
        mean_f = sb("mean_f", [P, 2], F32, c)
        mean_sq = sb("mean_sq", [P, 2], BF16, c)
        psT = pb("psTa", [P, DC, BLK], F32, c)
        psQ = [pb(f"psQ{i}", [P, BLK], F32, c) for i in range(2)]
        psV = [pb(f"psV{i}", [P, D], F32, c) for i in range(2)]
        psN = [pb(f"psN{i}", [NH, BLK], F32, c) for i in range(2)]

        with nc.Block() as block:
            @block.sync
            def _(sp):
                sp.dma_start(raw[:, 0:NQ, :], a["qkv_w"].rearrange("(b p) d -> p b d", p=P)).then_inc(sem("raw"), 16)
                sp.dma_start(raw[:, NQ:, :], a["proj_w"].rearrange("(b p) d -> p b d", p=P)).then_inc(sem("raw"), 16)
                sp.dma_start(x_d.rearrange("(t p) d -> p t d", p=P), X).then_inc(sem("x_kept"), 16)
                sp.dma_start(bias[:, :], a["qkv_b"][0:2 * D].rearrange("(b p) -> p b", p=P),
                             allow_slow_non_contiguous=True).then_inc(sem("bias"), 16)
                sp.dma_start(vbias[:, :], a["qkv_b"][2 * D:3 * D].partition_broadcast(P)).then_inc(sem("bias"), 16)
                for r in range(2):
                    sp.sem_inc(sem(f"part_stored{r}"), 16)
                with sp.Fori(0, NB) as b:
                    for e in range(NE):
                        sp.wait_ge(sem("split"), b * NE + (e + 1))
                        sp.dma_start(part_d[:, e * P:(e + 1) * P, bass.ds(b * BLK, BLK)].rearrange("a p t -> p a t"),
                                     parts[:, e % 2, :, :]).then_inc(sem(f"part_stored{e % 2}"), 16)
                for r in range(2):
                    sp.wait_ge(sem(f"part_stored{r}"), 16 * (1 + NB * NE // 2))
                sp.wait_ge(sem("x_kept"), 16)

            @block.gpsimd
            def _(pool):
                pool.memset(heads[:, :, :], 1.0).then_inc(sem("heads"), 1)
                pool.wait_ge(sem("heads"), 1)
                pool.affine_select(out=heads[:, :, :], in_=heads[:, :, :], compare_op=ALU.is_ge, fill=0.0,
                                   base=0, pattern=[[P, 2], [-HD, NH]], channel_multiplier=1).then_inc(sem("heads"), 1)
                pool.wait_ge(sem("heads"), 2)
                pool.affine_select(out=heads[:, :, :], in_=heads[:, :, :], compare_op=ALU.is_ge, fill=0.0,
                                   base=HD - 1, pattern=[[-P, 2], [HD, NH]], channel_multiplier=-1).then_inc(sem("heads"), 1)

            @block.tensor
            def _(pe):
                pe.wait_ge(sem("raw"), 32)
                for b in range(NW):
                    if b >= 2:
                        pe.wait_ge(sem("w_out"), b - 1)
                    for c in range(DC):
                        last = pe.transpose(psQ[b % 2][:, c * P:(c + 1) * P], raw[:, b, c * P:(c + 1) * P], ident[:, :])
                    last.then_inc(sem("w_turned"), 1)
                pe.wait_ge(sem("w_out"), NW)
                pe.wait_ge(sem("heads"), 3)
                pe.sem_inc(sem("turned"), TPB)
                pe.sem_inc(sem("measured"), 1)

                def turn(j):
                    if has(j, 0, NB):
                        pe.wait_ge(sem("xnt_ready"), j + 1)
                    for u in range(TPB):
                        pe.wait_ge(sem("xn_ready"), j * TPB + (TPB + u + 1))
                        for c in range(DC):
                            last = pe.transpose(psT[:, c, u * P:(u + 1) * P], xn[:, u, c * P:(c + 1) * P], ident[:, :])
                        last.then_inc(sem("turned"), 1)

                def step(j, s, lap):
                    if has(j, 0, NB):
                        pe.wait_ge(sem("xnt_ready"), j + 1)
                        for u in range(TPB):
                            if not (isinstance(j, int) and j == 0 and u < 2):
                                pe.wait_ge(sem("v_out"), j * TPB + (u - 1))
                            for c in range(DC):
                                last = pe.matmul(psV[u % 2][:, :], xnt[:, s % 2, c, u * P:(u + 1) * P], wt[:, c, 2 * D:],
                                                 start=(c == 0), stop=(c == DC - 1))
                            last.then_inc(sem("v_in"), 1)
                    if has(j, -1, NB):
                        pe.wait_ge(sem("squared"), j * NE)
                        if has(j, -2, NB):
                            pe.wait_ge(sem("norm_out"), j - 1)
                        for n in range(2):
                            for b in range(2):
                                last = pe.matmul(psN[n][:, :], heads[:, b, :], square[:, 2 * n + b, :],
                                                 start=(b == 0), stop=(b == 1))
                        last.then_inc(sem("measured"), 1)
                    if has(j, 0, NB):
                        for e in range(NE):
                            if not (isinstance(j, int) and j == 0 and e < 2):
                                pe.wait_ge(sem("q_out"), j * NE + (e - 1))
                            for c in range(DC):
                                last = pe.matmul(psQ[e % 2][:, :], wt[:, c, e * P:(e + 1) * P], xnt[:, s % 2, c, :],
                                                 start=(c == 0), stop=(c == DC - 1))
                            last.then_inc(sem("q_in"), 1)
                            if e == 1 and has(j, 1, NB):
                                turn(j)
                    elif has(j, 1, NB):
                        turn(j)

                skewed(pe, NB, 2, step)
                pe.wait_ge(sem("mean_sq"), 1)
                for b in range(2):
                    last = pe.matmul(psN[0][:, 0:1], heads[:, b, :], mean_sq[:, b:b + 1], start=(b == 0), stop=(b == 1))
                last.then_inc(sem("mean_in"), 1)

            @block.scalar
            def _(act):
                for b in range(NW):
                    act.wait_ge(sem("w_turned"), b + 1)
                    dst = wt[:, :, b * P:(b + 1) * P] if b < NQ else pwt[:, :, (b - NQ) * P:(b - NQ + 1) * P]
                    act.activation(dst, psQ[b % 2][:, 0:D].rearrange("p (c q) -> p c q", c=DC), ACT.Copy).then_inc(sem("w_out"), 1)
                act.wait_ge(sem("sqrt"), 1)
                act.activation(tmp[:, :], var[:, :], ACT.Sqrt).then_inc(sem("sqrt"), 1)
                act.wait_ge(sem("bias"), 32)

                def turned(j, s):
                    act.wait_ge(sem("turned"), j * TPB + 3 * TPB)
                    if has(j, -1, NB):
                        act.wait_ge(sem("q_in"), j * NE)
                    for c in range(DC):
                        last = act.activation(xnt[:, (s + 1) % 2, c, :], psT[:, c, :], ACT.Copy)
                    last.then_inc(sem("xnt_ready"), 1)

                def step(j, s, lap):
                    if has(j, 0, NB):
                        for e in range(NE):
                            act.wait_ge(sem("q_in"), j * NE + (e + 1))
                            act.wait_ge(sem(f"part_stored{e % 2}"), (j * (NE // 2) + e // 2) * 16 + 16)
                            act.activation(parts[:, e % 2, 0, :], psQ[e % 2][:, :], ACT.Identity, bias=bias[:, e:e + 1])
                            total = key_sum[:, e - 2, bass.ds(j, 1)] if e >= 2 else None
                            act.activation(full[:, e % 2, :], psQ[e % 2][:, :], ACT.Identity, bias=bias[:, e:e + 1],
                                           accum_out=total)\
                               .then_inc(sem("q_out"), 1)
                            act.wait_ge(sem("q_out"), j * NE + (e + 1))
                            if e == 0:
                                act.wait_ge(sem("measured"), j + 1)
                            act.activation(square[:, e, :], full[:, e % 2, :], ACT.Square).then_inc(sem("squared"), 1)
                            if e == 1 and has(j, 1, NB):
                                turned(j, s)
                    elif has(j, 1, NB):
                        turned(j, s)

                skewed(act, NB, 2, step)

            @block.vector
            def _(v):
                own = Chain(v, sem("dve"))
                normalise_stats(v, own.link, X, stats, mean, rstd, tmp, var, sem("stats"), sem("sqrt"))
                v.wait_ge(sem("bias"), 32)

                def step(j, s, lap):
                    if has(j, 0, NB):
                        for u in range(TPB):
                            t = j * TPB + u
                            v.wait_ge(sem("v_in"), t + 1)
                            v.tensor_tensor(V[:, t, :], psV[u % 2][:, :], vbias[:, :], ALU.add).then_inc(sem("v_out"), 1)
                    if has(j, 1, NB):
                        for u in range(TPB):
                            t = j * TPB + (TPB + u)
                            v.wait_ge(sem("turned"), t + 1)
                            v.tensor_scalar(xn[:, u, :], X[:, t, :], mean[:, bass.ds(t, 1)], rstd[:, bass.ds(t, 1)],
                                            ALU.subtract, ALU.mult).then_inc(sem("xn_ready"), 1)
                    if has(j, -1, NB):
                        v.wait_ge(sem("measured"), j + 1)
                        v.tensor_scalar(norms[:, bass.ds((j - 1) * BLK, BLK)], psN[0][:, :], 1.0, None, ALU.mult)
                        v.tensor_reduce(key_norm[:, bass.ds(j - 1, 1)], psN[1][:, :], AX, ALU.max).then_inc(sem("norm_out"), 1)
                    if has(j, 0, NB):
                        for e in range(NE):
                            n = j * NE + e
                            f, r, g = full[:, e % 2, :], rest[:, :], parts[:, e % 2, :, :]
                            v.wait_ge(sem("q_out"), n + 1)
                            if not (isinstance(n, int) and n == 0):
                                v.wait_ge(sem("split"), n)
                            v.tensor_tensor(r, f, g[:, 0, :], ALU.subtract).then_inc(sem("rest"), 1)
                            v.wait_ge(sem("rest"), n + 1)
                            v.tensor_copy(g[:, 1, :], r).then_inc(sem("mid"), 1)
                            v.wait_ge(sem("mid"), n + 1)
                            v.tensor_tensor(g[:, 2, :], r, g[:, 1, :], ALU.subtract).then_inc(sem("split"), 1)

                skewed(v, NB, 2, step)
                own.link(v.tensor_reduce(mean_f[:, :], key_sum[:, :, :], AX, ALU.add))
                own.link(v.tensor_scalar(mean_f[:, :], mean_f[:, :], 1.0 / T, None, ALU.mult))
                v.tensor_tensor(mean_sq[:, :], mean_f[:, :], mean_f[:, :], ALU.mult).then_inc(sem("mean_sq"), 1)
                v.wait_ge(sem("mean_in"), 1)
                own.link(v.tensor_copy(key_mean[:, :], psN[0][:, 0:1]))


def bound_shift(nc, sem, sb, pb, ident, norms, key_norm, key_mean, safe, shift_d):
    with ExitStack() as c:
        far = sb("far", [NH, 1], F32, c)
        shift = sb("shift", [NH, T], BF16, c)
        zero = sb("zero_shift", [NH, T], BF16, c)
        worst = sb("worst", [NH, 1], F32, c)
        long = sb("long", [NH, 1], F32, c)
        below = sb("below", [NH, 1], F32, c)
        worst1 = sb("worst1", [1, 1], F32, c)
        psF = pb("psF", [1, NH], F32, c)
        with nc.Block() as block:
            @block.vector
            def _(v):
                own = Chain(v, sem("dve_b"))
                v.memset(zero[:, :], 0.0).then_inc(sem("zeroed"), 1)
                own.link(v.tensor_reduce(far[:, :], key_norm[:, :], AX, ALU.max))
                own.link(v.tensor_reduce(long[:, :], norms[:, :], AX, ALU.max))
                own.link(v.tensor_scalar(long[:, :], long[:, :], key_mean[:, :], 1.1, ALU.mult, ALU.mult))
                v.tensor_scalar(far[:, :], far[:, :], 1.1 / 4, None, ALU.mult).then_inc(sem("far"), 1)
                v.wait_ge(sem("bounded"), 2)
                own.link(v.tensor_reduce(worst[:, :], shift[:, :], AX, ALU.max))
                own.link(v.tensor_tensor(worst[:, :], worst[:, :], below[:, :], ALU.add))
                v.tensor_scalar(shift[:, :], shift[:, :], -1.0, None, ALU.mult).then_inc(sem("negated"), 1)
                v.sem_inc(sem("worst"), 1)
                v.wait_ge(sem("worst_row"), 1)
                own.link(v.tensor_reduce(worst1[:, :], psF[:, :], AX, ALU.max))
                own.link(v.tensor_scalar(safe[:, :], worst1[:, :], LIMIT, None, ALU.is_le))

            @block.scalar
            def _(act):
                act.wait_ge(sem("far"), 1)
                act.activation(shift[:, :], norms[:, :], ACT.Sqrt, scale=far[:, :]).then_inc(sem("bounded"), 1)
                act.activation(below[:, :], long[:, :], ACT.Sqrt).then_inc(sem("bounded"), 1)

            @block.tensor
            def _(pe):
                pe.wait_ge(sem("negated"), 1)
                pe.transpose(psF[:, :], worst[:, :], ident[0:NH, 0:NH]).then_inc(sem("worst_row"), 1)

            @block.sync
            def _(sp):
                sp.wait_ge(sem("zeroed"), 1)
                for n in range(1, NPART):
                    sp.dma_start(shift_d[n], zero[:, :]).then_inc(sem("shift_out"), 16)
                sp.wait_ge(sem("negated"), 1)
                sp.dma_start(shift_d[0], shift[:, :]).then_inc(sem("shift_out"), 16)
                sp.wait_ge(sem("shift_out"), 16 * NPART)


def query_rows(sp, dst, part_d, h, signal):
    row = 0
    for part, times in ((0, 3), (1, 2), (2, 1)):
        for _ in range(times):
            sp.dma_start(dst[row:row + HD, :], part_d[part, bass.ds(h * HD, HD), :]).then_inc(signal, 16)
            row += HD


def key_rows(sp, dst, part_d, h, signal):
    for n, part in enumerate((0, 1, 2, 0, 1, 0)):
        sp.dma_start(dst[n * HD:(n + 1) * HD, :], part_d[part, bass.ds(h * HD + D, HD), :]).then_inc(signal, 16)


def exact_shift(nc, sem, sb, pb, RA, ident, safe, part_d, shift_d):
    ops = RA[:, :].bitcast(BF16).rearrange("p (n t) -> p n t", n=4)
    HALF = T // 2
    with ExitStack() as c:
        half = sb("half_max", [P, NT, 2], F32, c)
        most = sb("most", [P, NT], F32, c)
        neg = sb("neg_most", [NT, P], F32, c)
        rest = sb("neg_rest", [NT, P], F32, c)
        parts = sb("neg_parts", [NT, NPART, P], BF16, c)
        psS = [pb(f"psSx{i}", [P, HALF], F32, c) for i in range(2)]
        with nc.Block() as block:
            @block.sync
            def _(sp):
                ok = sp.value_load(safe[0:1, 0:1], min_val=0, max_val=1)
                with sp.If(ok < 1):
                    with sp.Fori(0, NH) as h:
                        sp.wait_ge(sem("x_free"), h + 1)
                        carried(sp, sem("x_seen_sp"))
                        query_rows(sp, ops[:, 0, :], part_d, h, sem("x_ops"))
                        key_rows(sp, ops[:, 1, :], part_d, h, sem("x_ops"))
                        sp.wait_ge(sem("x_split"), h + 1)
                        carried(sp, sem("x_seen_sp"))
                        sp.dma_start(shift_d[:, bass.ds(h, 1), :].rearrange("a h (t p) -> (h t) a p", p=P), parts[:, :, :])\
                          .then_inc(sem("x_shift"), 16)
                        sp.wait_ge(sem("x_shift"), h * 16 + 16)
                        carried(sp, sem("x_seen_sp"))

            @block.tensor
            def _(pe):
                ok = pe.value_load(safe[0:1, 0:1], min_val=0, max_val=1)
                with pe.If(ok < 1):
                    pe.sem_inc(sem("x_free"), 1)
                    with pe.Fori(0, NH) as h:
                        pe.wait_ge(sem("x_ops"), h * (16 * 12) + 16 * 12)
                        carried(pe, sem("x_seen_pe"))
                        with pe.Fori(0, NT) as t:
                            for n in range(2):
                                pe.wait_ge(sem("x_read"), (h * NT + t) * 2 + (n + 1))
                                for b in range(HALF // BLK):
                                    last = pe.matmul(psS[n][:, b * BLK:(b + 1) * BLK], ops[0:KROWS, 0, bass.ds(t * P, P)],
                                                     ops[0:KROWS, 1, n * HALF + b * BLK:n * HALF + (b + 1) * BLK],
                                                     start=True, stop=True)
                                last.then_inc(sem("x_scores"), 1)
                        pe.wait_ge(sem("x_most"), h + 1)
                        pe.transpose(psS[0][0:NT, 0:P], most[:, :], ident[:, :]).then_inc(sem("x_turned"), 1)
                        pe.sem_inc(sem("x_free"), 1)

            @block.vector
            def _(v):
                ok = v.value_load(safe[0:1, 0:1], min_val=0, max_val=1)
                with v.If(ok < 1):
                    v.sem_inc(sem("x_read"), 2)
                    with v.Fori(0, NH) as h:
                        with v.Fori(0, NT) as t:
                            for n in range(2):
                                k = (h * NT + t) * 2 + n
                                v.wait_ge(sem("x_scores"), k + 1)
                                v.tensor_reduce(half[:, bass.ds(t, 1), n], psS[n][:, :], AX, ALU.max).then_inc(sem("x_read"), 1)
                        v.wait_ge(sem("x_read"), h * (2 * NT) + (2 * NT + 2))
                        v.tensor_tensor(most[:, :], half[:, :, 0], half[:, :, 1], ALU.max).then_inc(sem("x_most"), 1)
                        v.wait_ge(sem("x_turned"), h + 1)
                        v.tensor_scalar(neg[:, :], psS[0][0:NT, 0:P], -1.0, None, ALU.mult).then_inc(sem("x_neg"), 1)
                        v.wait_ge(sem("x_neg"), h * 4 + 1)
                        v.tensor_copy(parts[:, 0, :], neg[:, :]).then_inc(sem("x_neg"), 1)
                        v.wait_ge(sem("x_neg"), h * 4 + 2)
                        v.tensor_tensor(rest[:, :], neg[:, :], parts[:, 0, :], ALU.subtract).then_inc(sem("x_neg"), 1)
                        v.wait_ge(sem("x_neg"), h * 4 + 3)
                        v.tensor_copy(parts[:, 1, :], rest[:, :]).then_inc(sem("x_neg"), 1)
                        v.wait_ge(sem("x_neg"), h * 4 + 4)
                        v.tensor_tensor(parts[:, 2, :], rest[:, :], parts[:, 1, :], ALU.subtract).then_inc(sem("x_split"), 1)
                        v.wait_ge(sem("x_shift"), h * 16 + 16)


def attend(nc, sem, sb, pb, RA, V, part_d, shift_d, head_d):
    ops = RA[:, :].bitcast(BF16).rearrange("p (n t) -> p n t", n=4)
    Q, K = [ops[:, 2 * r, :] for r in range(2)], [ops[:, 2 * r + 1, :] for r in range(2)]
    KT = NT
    QU = T // (4 * BLK)
    W = 2 * BLK
    CH = 4 * BLK // W
    STEPS = 2 * QU * KT
    SLOTS, PS = 3, 4
    CREDIT = 4
    n_chunks = STEPS * CH
    slots = [n % SLOTS for n in range(n_chunks)]
    slots[-4:] = [0, 1, 2, 1]
    LOADS = 13

    def since(n):
        d = 1
        while slots[(n - d) % n_chunks] != slots[n]:
            d += 1
        return d

    with ExitStack() as c:
        values = sb("values", [P, 2, KT, 2 * HD], F32, c)
        probs = sb("probs", [P, PS, W], F32, c)
        sums = sb("sums", [P, 2, BLK], F32, c)
        inverse = sb("inverse", [P, 2, BLK], F32, c)
        psS = [pb(f"psS{i}", [P, W], F32, c) for i in range(SLOTS)]
        psO = [pb(f"psO_{i}", [P, BLK], F32, c) for i in range(2)]

        def rounds(eng, body):
            with eng.Fori(0, NH // 2 - 1) as r:
                body(r, False)
            body(NH // 2 - 1, True)

        with nc.Block() as block:
            @block.gpsimd
            def _(pool):
                for r in range(2):
                    pool.memset(values[:, r, :, 0:HD], 1.0).then_inc(sem("ones"), 1)
                    pool.wait_ge(sem("ones"), 2 * r + 1)
                    pool.memset(K[r][KROWS:QROWS, :], 1.0).then_inc(sem("ones"), 1)
                    pool.wait_ge(sem("ones"), 2 * r + 2)

            @block.sync
            def _(sp):
                def load(h, r):
                    query_rows(sp, Q[r], part_d, h, sem(f"ops{r}"))
                    sp.dma_start(Q[r][KROWS:QROWS, :], shift_d[:, bass.ds(h, 1), :].rearrange("a h t -> (a h) t"))\
                      .then_inc(sem(f"ops{r}"), 16)
                    key_rows(sp, K[r], part_d, h, sem(f"ops{r}"))

                for r in range(2):
                    load(r, r)

                def body(r2, last):
                    for r in range(2):
                        h = r2 * 2 + r
                        for q in range(QU):
                            g = h * QU + q
                            sp.wait_ge(sem("inverted"), g + 1)
                            carried(sp, sem("seen_sp"))
                            for j in range(4):
                                for s, rows in enumerate((inverse, sums)):
                                    sp.dma_start(head_d[4 * q + j, s, bass.ds(h * HD, HD), :],
                                                 rows[32 * j + HD * s:32 * j + HD * (s + 1), q % 2, :])\
                                      .then_inc(sem(f"o_stored{q % 2}"), 16)
                        if not last:
                            sp.wait_ge(sem("pv"), h * (QU * KT) + (QU * KT + 2))
                            carried(sp, sem("seen_sp"))
                            load(h + 2, r)

                rounds(sp, body)
                for q in range(2):
                    sp.wait_ge(sem(f"o_stored{q}"), 16 * 8 * (NH * QU // 2 + 1))

            @block.tensor
            def _(pe):
                pe.wait_ge(sem("ones"), 4)
                pe.sem_inc(sem("pv"), 2)

                def scores(r2, m):
                    k, n = m // CH, m % CH
                    r, q, kt = k // (QU * KT), k // KT % QU, k % KT
                    if q == 0 and kt == 0 and n == 0:
                        pe.wait_ge(sem(f"ops{r}"), r2 * (16 * LOADS) + 16 * LOADS)
                    pe.wait_ge(sem("exped"), r2 * n_chunks + (m - since(m) + 1 + CREDIT))
                    for b in range(W // BLK):
                        at = (q * 4 + n * (W // BLK) + b) * BLK
                        last = pe.matmul(psS[slots[m]][:, b * BLK:(b + 1) * BLK], K[r][0:QROWS, kt * P:(kt + 1) * P],
                                         Q[r][0:QROWS, at:at + BLK], start=True, stop=True)
                    last.then_inc(sem("scored"), 1)

                def weigh(r2, k):
                    r, q, kt = k // (QU * KT), k // KT % QU, k % KT
                    if kt == 0:
                        pe.wait_ge(sem("o_out"), r2 * (2 * QU) + (r * QU + q + 1))
                        if q == 0:
                            pe.wait_ge(sem("filled"), r2 * 2 + (r + 1))
                    pe.wait_ge(sem("exped"), r2 * n_chunks + ((k + 1) * CH + CREDIT))
                    for j in range(4):
                        m = k * CH + j * BLK // W
                        at = j * BLK % W
                        last = pe.matmul(psO[q % 2][32 * j:32 * (j + 1), :], values[:, r, kt, :],
                                         probs[:, m % PS, at:at + BLK], start=(kt == 0), stop=(kt == KT - 1))
                    last.then_inc(sem("pv"), 1)

                def ahead(r2, m, last):
                    if m < n_chunks:
                        scores(r2, m)
                    elif not last:
                        scores(r2 + 1, m - n_chunks)

                def body(r2, last):
                    for k in range(STEPS):
                        ahead(r2, (k + 2) * CH, last)
                        weigh(r2, k)
                        ahead(r2, (k + 2) * CH + 1, last)

                for m in range(2 * CH):
                    scores(0, m)
                rounds(pe, body)

            @block.scalar
            def _(act):
                act.sem_inc(sem("exped"), CREDIT)

                def body(r2, last):
                    for m in range(n_chunks):
                        act.wait_ge(sem("scored"), r2 * n_chunks + (m + 1))
                        if m % CH == 0:
                            act.wait_ge(sem("pv"), r2 * STEPS + (m // CH + 1))
                        act.activation(probs[:, m % PS, :], psS[slots[m]][:, :], ACT.Exp, scale=SCALE).then_inc(sem("exped"), 1)

                rounds(act, body)

            @block.vector
            def _(v):
                def fill(h, r):
                    v.tensor_copy(values[:, r, :, HD:], V[:, :, bass.ds(h * HD, HD)]).then_inc(sem("filled"), 1)

                for q in range(2):
                    v.sem_inc(sem(f"o_stored{q}"), 16 * 8)
                v.sem_inc(sem("o_out"), 2)
                for r in range(2):
                    fill(r, r)

                def body(r2, last):
                    for r in range(2):
                        h = r2 * 2 + r
                        for q in range(QU):
                            g = h * QU + q
                            v.wait_ge(sem("pv"), g * KT + (KT + 2))
                            v.wait_ge(sem(f"o_stored{q % 2}"), h * (16 * 8) + 16 * 8)
                            v.tensor_copy(sums[:, q % 2, :], psO[q % 2][:, :]).then_inc(sem("o_out"), 1)
                            v.wait_ge(sem("o_out"), g + 3)
                            v.reciprocal(inverse[:, q % 2, :], sums[:, q % 2, :]).then_inc(sem("inverted"), 1)
                        if not last:
                            fill(h + 2, r)

                rounds(v, body)


def project_out(nc, a, sem, sb, pb, X, pwt, x_d, head_d):
    with ExitStack() as c:
        hd = sb("hd", [P, 2, 2, DC, BLK], F32, c)
        norm = sb("norm", [P, 2, DC, BLK], F32, c)
        pbias = sb("pbias", [P, D], F32, c)
        psP = [pb(f"psP{i}", [P, D], F32, c) for i in range(4)]
        with nc.Block() as block:
            @block.sync
            def _(sp):
                sp.dma_start(pbias[:, :], a["proj_b"].partition_broadcast(P)).then_inc(sem("pbias"), 16)
                for b in range(NB):
                    w = b % 2
                    if b >= 2:
                        sp.wait_ge(sem("divided"), b - 1)
                    for s in range(2):
                        sp.dma_start(hd[:, w, s, :, :], head_d[b, s, :, :].rearrange("(c p) q -> p c q", p=P))\
                          .then_inc(sem(f"hd{w}"), 16)

            @block.scalar
            def _(act):
                for b in range(NB):
                    act.dma_start(X[:, b * TPB:(b + 1) * TPB, :],
                                  x_d[b * BLK:(b + 1) * BLK, :].rearrange("(t p) d -> p t d", p=P))\
                       .then_inc(sem(f"x_back{b}"), 16)

            @block.gpsimd
            def _(pool):
                pool.wait_ge(sem("pbias"), 16)
                for b in range(NB):
                    pool.wait_ge(sem(f"x_back{b}"), 16)
                    pool.tensor_tensor(X[:, b * TPB:(b + 1) * TPB, :], X[:, b * TPB:(b + 1) * TPB, :],
                                       pbias[:, :].unsqueeze(1).to_broadcast([P, TPB, D]), ALU.add).then_inc(sem("biased"), 1)

            @block.vector
            def _(v):
                for b in range(NB + 1):
                    w = b % 2
                    if b < NB:
                        v.wait_ge(sem(f"hd{w}"), (b // 2) * 32 + 32)
                        if b >= 2:
                            v.wait_ge(sem("projected"), (b - 1) * TPB)
                        v.tensor_tensor(norm[:, w, :, :], hd[:, w, 1, :, :], hd[:, w, 0, :, :], ALU.mult)\
                         .then_inc(sem("divided"), 1)
                    if b >= 1:
                        v.wait_ge(sem("biased"), b)
                        for u in range(TPB):
                            t = (b - 1) * TPB + u
                            v.wait_ge(sem("projected"), t + 1)
                            v.tensor_tensor(X[:, t, :], psP[u][:, :], X[:, t, :], ALU.add).then_inc(sem("p_out"), 1)
                v.wait_ge(sem("p_out"), NT)

            @block.tensor
            def _(pe):
                for b in range(NB):
                    w = b % 2
                    pe.wait_ge(sem("divided"), b + 1)
                    for u in range(TPB):
                        if b >= 1:
                            pe.wait_ge(sem("p_out"), (b - 1) * TPB + (u + 1))
                        for c in range(DC):
                            last = pe.matmul(psP[u][:, :], norm[:, w, c, u * P:(u + 1) * P], pwt[:, c, :],
                                             start=(c == 0), stop=(c == DC - 1))
                        last.then_inc(sem("projected"), 1)


def ffn_out(nc, a, out, env):
    sem, X = env["sem"], env["X"]
    with nc.Block() as block:
        @block.sync
        def _(sp):
            sp.dma_start(out[0].rearrange("(t p) d -> p t d", p=P), X).then_inc(sem("out"), 16)
            sp.wait_ge(sem("out"), 16)


NAMES = {"x": "L0_attn_x", "qkv_w": "L0_attn_qkv_w", "qkv_b": "L0_attn_qkv_b", "proj_w": "L0_attn_proj_w",
         "proj_b": "L0_attn_proj_b", "Wg": "L0_ffn_Wg", "W1": "L0_ffn_W1", "W2": "L0_ffn_W2", "W3": "L0_ffn_W3",
         "Ws1": "L0_ffn_Ws1", "Ws2": "L0_ffn_Ws2", "Ws3": "L0_ffn_Ws3"}


def kernel(**inputs):
    import concourse.bacc as bacc
    from concourse.bass_utils import run_bass_kernel_spmd

    nc = bacc.Bacc("TRN2", target_bir_lowering=False, num_devices=1)
    arrays, aps = {}, {}
    for short, name in NAMES.items():
        v = np.ascontiguousarray(inputs[name])
        arrays[f"in_{short}"] = v
        aps[short] = nc.dram_tensor(f"in_{short}", v.shape, mybir.dt.from_np(v.dtype), kind="ExternalInput").ap()
    out = nc.dram_tensor("out_x", (1, T, D), F32, kind="ExternalOutput").ap()
    build(nc, aps, out)
    return run_bass_kernel_spmd(nc, [arrays], core_ids=[0]).results[0]["out_x"]
```
